# Optimizing a Trainium2 kernel written in Bass

```python
import numpy as np
import jax
import jax.numpy as jnp

def _softmax(x, axis=-1):
    return jax.nn.softmax(x, axis=axis)

def _gelu(x):
    return jax.nn.gelu(x, approximate=True)

def _silu(x):
    return jax.nn.silu(x)

def _sigmoid(x):
    return jax.nn.sigmoid(x)

def _layernorm(x, axis=-1, eps=1e-05):
    m = jnp.mean(x, axis=axis, keepdims=True)
    v = jnp.var(x, axis=axis, keepdims=True)
    return (x - m) / jnp.sqrt(v + eps)

def _scatter_add(tgt, idx, src, axis=0):
    return tgt.at[idx].add(src)

def _segment_sum(src, seg, n):
    return jax.ops.segment_sum(src, seg, n)
kernel_name = 'mk_conv_seq_d2_conv_nchw512_r2_9a7dbc'

def setup_inputs(seed: int=0):
    np.random.seed(seed)
    _w = jnp.asarray

    def _rec_inputs():
        import jax
        import jax.numpy as jnp
        _gk = jax.random.key(seed)
        x = -0.0002928 + 1 * jax.random.normal(jax.random.fold_in(_gk, 1), (8, 256, 32, 32), jnp.float32)
        return x
    x = _rec_inputs()

    def _L0_conv_setup():
        import jax, jax.numpy as jnp
        import numpy as np
        ALPHA = 32.0 ** 2
        HEADS = 8
        DIM_HEAD = 32
        EPS = 1e-05

        def _leaky(x):
            return jnp.where(x >= 0, x, 0.1 * x)

        def _cpb_bias(fmap_size, w0, b0, w1, b1, w2, b2):
            pos = jnp.arange(fmap_size)
            gi, gj = jnp.meshgrid(pos, pos, indexing='ij')
            grid = jnp.stack([gi, gj], axis=-1).reshape(-1, 2)
            rel = grid[:, None, :] - grid[None, :, :]
            rel = jnp.sign(rel) * jnp.log(jnp.abs(rel) + 1.0)
            h = _leaky(jnp.einsum('ijc,dc->ijd', rel.astype(jnp.float32), w0) + b0)
            h = _leaky(jnp.einsum('ijc,dc->ijd', h, w1) + b1)
            h = jnp.einsum('ijc,hc->ijh', h, w2) + b2
            return jnp.transpose(h, (2, 0, 1))

        def _stable_softmax(t, alpha=ALPHA):
            t = t / alpha
            t = t - jax.lax.stop_gradient(jnp.max(t, axis=-1, keepdims=True))
            return jax.nn.softmax(t * alpha, axis=-1)
        key = jax.random.key(seed)
        ks = jax.random.split(key, 9)
        B, C, H, W = (8, 256, 32, 32)
        inner = HEADS * DIM_HEAD
        s = 0.05
        return {'x': jax.random.normal(ks[0], (B, C, H, W), jnp.float32), 'gamma': jnp.ones((1, C, 1, 1), jnp.float32), 'w_qkv': jax.random.normal(ks[1], (inner * 3, C), jnp.float32) * s, 'w_out': jax.random.normal(ks[2], (C, inner), jnp.float32) * s, 'cpb_w0': jax.random.normal(ks[3], (64, 2), jnp.float32) * s, 'cpb_b0': jax.random.normal(ks[4], (64,), jnp.float32) * s, 'cpb_w1': jax.random.normal(ks[5], (64, 64), jnp.float32) * s, 'cpb_b1': jax.random.normal(ks[6], (64,), jnp.float32) * s, 'cpb_w2': jax.random.normal(ks[7], (HEADS, 64), jnp.float32) * s, 'cpb_b2': jax.random.normal(ks[8], (HEADS,), jnp.float32) * s}
    _L0_conv_all = _L0_conv_setup()
    _L0_conv_in = {k: v for k, v in _L0_conv_all.items() if k in ('gamma', 'w_qkv', 'w_out', 'cpb_w0', 'cpb_b0', 'cpb_w1', 'cpb_b1', 'cpb_w2', 'cpb_b2')}
    del _L0_conv_all

    def _L1_conv_setup():
        import jax, jax.numpy as jnp
        import numpy as np
        B, C, H, W = (4, 256, 32, 32)
        C8 = C // 8
        key = jax.random.key(seed)
        ks = jax.random.split(key, 8)
        return {'x': jax.random.normal(ks[0], (B, C, H, W), dtype=jnp.float32), 'Wf': jax.random.normal(ks[1], (C8, C), dtype=jnp.float32) * (1.0 / np.sqrt(C)), 'bf': jax.random.normal(ks[2], (C8,), dtype=jnp.float32) * 0.02, 'Wg': jax.random.normal(ks[3], (C8, C), dtype=jnp.float32) * (1.0 / np.sqrt(C)), 'bg': jax.random.normal(ks[4], (C8,), dtype=jnp.float32) * 0.02, 'Wh': jax.random.normal(ks[5], (C, C), dtype=jnp.float32) * (1.0 / np.sqrt(C)), 'bh': jax.random.normal(ks[6], (C,), dtype=jnp.float32) * 0.02, 'gamma': jax.random.normal(ks[7], (1,), dtype=jnp.float32)}
    _L1_conv_all = _L1_conv_setup()
    _L1_conv_in = {k: v for k, v in _L1_conv_all.items() if k in ('Wf', 'bf', 'Wg', 'bg', 'Wh', 'bh', 'gamma')}
    del _L1_conv_all
    return {'x': x, 'L0_conv_gamma': _L0_conv_in['gamma'], 'L0_conv_w_qkv': _L0_conv_in['w_qkv'], 'L0_conv_w_out': _L0_conv_in['w_out'], 'L0_conv_cpb_w0': _L0_conv_in['cpb_w0'], 'L0_conv_cpb_b0': _L0_conv_in['cpb_b0'], 'L0_conv_cpb_w1': _L0_conv_in['cpb_w1'], 'L0_conv_cpb_b1': _L0_conv_in['cpb_b1'], 'L0_conv_cpb_w2': _L0_conv_in['cpb_w2'], 'L0_conv_cpb_b2': _L0_conv_in['cpb_b2'], 'L1_conv_Wf': _L1_conv_in['Wf'], 'L1_conv_bf': _L1_conv_in['bf'], 'L1_conv_Wg': _L1_conv_in['Wg'], 'L1_conv_bg': _L1_conv_in['bg'], 'L1_conv_Wh': _L1_conv_in['Wh'], 'L1_conv_bh': _L1_conv_in['bh'], 'L1_conv_gamma': _L1_conv_in['gamma']}

def reference(x, L0_conv_gamma, L0_conv_w_qkv, L0_conv_w_out, L0_conv_cpb_w0, L0_conv_cpb_b0, L0_conv_cpb_w1, L0_conv_cpb_b1, L0_conv_cpb_w2, L0_conv_cpb_b2, L1_conv_Wf, L1_conv_bf, L1_conv_Wg, L1_conv_bg, L1_conv_Wh, L1_conv_bh, L1_conv_gamma):
    import jax
    import jax.numpy as jnp

    def _L0_conv_ref(x, gamma, w_qkv, w_out, cpb_w0, cpb_b0, cpb_w1, cpb_b1, cpb_w2, cpb_b2):
        import jax, jax.numpy as jnp
        import numpy as np
        ALPHA = 32.0 ** 2
        HEADS = 8
        DIM_HEAD = 32
        EPS = 1e-05

        def _leaky(x):
            return jnp.where(x >= 0, x, 0.1 * x)

        def _cpb_bias(fmap_size, w0, b0, w1, b1, w2, b2):
            pos = jnp.arange(fmap_size)
            gi, gj = jnp.meshgrid(pos, pos, indexing='ij')
            grid = jnp.stack([gi, gj], axis=-1).reshape(-1, 2)
            rel = grid[:, None, :] - grid[None, :, :]
            rel = jnp.sign(rel) * jnp.log(jnp.abs(rel) + 1.0)
            h = _leaky(jnp.einsum('ijc,dc->ijd', rel.astype(jnp.float32), w0) + b0)
            h = _leaky(jnp.einsum('ijc,dc->ijd', h, w1) + b1)
            h = jnp.einsum('ijc,hc->ijh', h, w2) + b2
            return jnp.transpose(h, (2, 0, 1))

        def _stable_softmax(t, alpha=ALPHA):
            t = t / alpha
            t = t - jax.lax.stop_gradient(jnp.max(t, axis=-1, keepdims=True))
            return jax.nn.softmax(t * alpha, axis=-1)
        B, C, H, W = x.shape
        n = H * W
        scale = DIM_HEAD ** (-0.5)
        residual = x
        mean = jnp.mean(x, axis=1, keepdims=True)
        var = jnp.var(x, axis=1, keepdims=True)
        xn = (x - mean) / jnp.sqrt(var + EPS) * gamma
        xf = xn.reshape(B, C, n)
        qkv = jnp.einsum('oc,bcn->bon', w_qkv, xf)
        q, k, v = jnp.split(qkv, 3, axis=1)
        rs = lambda t: t.reshape(B, HEADS, DIM_HEAD, n)
        q, k, v = (rs(q), rs(k), rs(v))
        sim = jnp.einsum('bhdi,bhdj->bhij', q, k) * scale
        bias = _cpb_bias(H, cpb_w0, cpb_b0, cpb_w1, cpb_b1, cpb_w2, cpb_b2)
        sim = sim + bias[None]
        attn = _stable_softmax(sim)
        out = jnp.einsum('bhij,bhdj->bhdi', attn, v)
        out = out.reshape(B, HEADS * DIM_HEAD, n)
        out = jnp.einsum('oc,bcn->bon', w_out, out).reshape(B, C, H, W)
        return out + residual

    def _L1_conv_ref(x, Wf, bf, Wg, bg, Wh, bh, gamma):
        import jax, jax.numpy as jnp
        import numpy as np
        B, C, H, W = (4, 256, 32, 32)
        C8 = C // 8
        b, c, h, w = x.shape
        n = h * w
        xf = x.reshape(b, c, n)
        f = jnp.einsum('oc,bcn->bno', Wf, xf) + bf
        g = jnp.einsum('oc,bcn->bon', Wg, xf) + bg[:, None]
        hh = jnp.einsum('oc,bcn->bon', Wh, xf) + bh[:, None]
        attn = jax.nn.softmax(jnp.einsum('bno,bom->bnm', f, g), axis=2)
        sa_map = jnp.einsum('bci,bij->bcj', hh, attn).reshape(b, c, h, w)
        return gamma * sa_map + x

    def _gn(v, G=32, eps=1e-05):
        B_, C_, H_, W_ = v.shape
        g = v.reshape(B_, G, C_ // G, H_, W_)
        m = jnp.mean(g, axis=(2, 3, 4), keepdims=True)
        s = jnp.var(g, axis=(2, 3, 4), keepdims=True)
        return ((g - m) / jnp.sqrt(s + eps)).reshape(v.shape)

    def _ln_c(v, eps=1e-06):
        m = jnp.mean(v, axis=1, keepdims=True)
        s = jnp.var(v, axis=1, keepdims=True)
        return (v - m) / jnp.sqrt(s + eps)

    def _ln_t(v, eps=1e-05):
        m = jnp.mean(v, axis=-1, keepdims=True)
        s = jnp.var(v, axis=-1, keepdims=True)
        return (v - m) / jnp.sqrt(s + eps)

    def _to_tokens(v):
        B_, C_, H_, W_ = v.shape
        return v.reshape(B_, C_, H_ * W_).transpose(0, 2, 1)

    def _from_tokens(t, like):
        B_, C_, H_, W_ = like.shape
        return t.transpose(0, 2, 1).reshape(B_, C_, H_, W_)
    x = _L0_conv_ref(x, L0_conv_gamma, L0_conv_w_qkv, L0_conv_w_out, L0_conv_cpb_w0, L0_conv_cpb_b0, L0_conv_cpb_w1, L0_conv_cpb_b1, L0_conv_cpb_w2, L0_conv_cpb_b2)
    x = _L1_conv_ref(x, L1_conv_Wf, L1_conv_bf, L1_conv_Wg, L1_conv_bg, L1_conv_Wh, L1_conv_bh, L1_conv_gamma)
    return x

_drawn_inputs = setup_inputs


def setup_inputs(seed=0):
    import zlib

    import numpy as np

    out = dict(_drawn_inputs(seed))
    spreads = {'L0_conv_gamma': (1.0, 0.6)}
    factors = {'L0_conv_cpb_w0': 8.0,
     'L0_conv_cpb_b0': 8.0,
     'L0_conv_cpb_w1': 8.0,
     'L0_conv_cpb_b1': 8.0,
     'L0_conv_cpb_w2': 8.0,
     'L0_conv_cpb_b2': 64.0,
     'L1_conv_bf': 23.835,
     'L1_conv_bg': 64.0,
     'L1_conv_bh': 21.955}
    for name, (base, spread) in spreads.items():
        noise = np.random.default_rng([zlib.crc32(name.encode()), seed]).standard_normal(out[name].shape)
        drawn = base * np.exp(spread * noise) if base else spread * noise
        out[name] = jnp.asarray(drawn.astype(out[name].dtype))
    for name, factor in factors.items():
        out[name] = (out[name] * factor).astype(out[name].dtype)
    return out
```

```python
from contextlib import ExitStack

import numpy as np

import concourse.bass as bass
from concourse import mybir

ALU = mybir.AluOpType
ACT = mybir.ActivationFunctionType
AX_X = mybir.AxisListType.X
F32 = mybir.dt.float32
F32R = mybir.dt.float32r

P = 128
HD = 32
HG = P // HD
EPS = 1e-5
LEAK = 0.1
BIG = 3.0e38
S_SLOTS = 4
P_GROUPS = 3
PV_LAG = 2


def two_layer_attention(nc, x, gamma, w_qkv, w_out, w0, b0, w1, b1, w2, b2,
                        Wf, bf, Wg, bg, Wh, bh, gamma1, rel_log, ident_in, out):
    B, C, H, W = x.shape
    N = H * W
    KC = C // P
    NT = N // P
    HALF = 512
    NHALF = N // HALF
    G = C // P
    ROWS = P // W
    DY, DX = 2 * H - 1, 2 * W - 1
    NA = H + (NT - 1) * ROWS
    D0 = w0.shape[0]
    SCALE = HD ** -0.5
    C8 = Wf.shape[0]
    KS = 3 * HD
    TG = NHALF * NT

    x_dram = x.rearrange("b (k p) h w -> b p k (h w)", p=P)
    out_dram = out.rearrange("b (k p) h w -> b p k (h w)", p=P)
    table_dram = nc.dram_tensor("bias_table", [G * HG, DY * DX], F32)
    lines_dram = nc.dram_tensor("bias_lines", [W, G * HG, DY, W], F32)

    with ExitStack() as ctx:
        def sb(name, shape, dt=F32):
            return ctx.enter_context(nc.sbuf_tensor(name, shape, dt))

        def sem(name):
            return ctx.enter_context(nc.semaphore(name))

        psum = ctx.enter_context(nc.psum_tensor("psum", [P, 8, HALF], F32))

        def pair(bank):
            return psum[:, bank:bank + 2, :].rearrange("p a b -> p (a b)")

        ident = sb("ident", [P, P])
        ones = sb("ones", [P, P])
        mean_w = sb("mean_w", [P, P])
        eps_col = sb("eps_col", [P, 1])
        wqkvT = sb("wqkvT", [P, KC, 3 * C])
        woutT = sb("woutT", [P, G, C])
        whT = sb("whT", [P, KC, C])
        wfgT = sb("wfgT", [P, KC, 2, KS])
        bfg = sb("bfg", [KS, 2])
        bh_all = sb("bh_all", [P, C])
        gamma_col = sb("gamma_col", [P, KC])
        gamma1_col = sb("gamma1_col", [P, 1])
        bias_lines = sb("bias_lines_sb", [P, G * HG, NA * W])
        xn = sb("xn", [P, KC, N])
        st_q = sb("st_q", [P, 2, N], F32R)
        st_k = sb("st_k", [P, 2, N], F32R)
        q_stack = sb("q_stack", [KS + 2, HG, N], F32R)
        k_stack = sb("k_stack", [KS + 2, HG, N], F32R)
        vT = sb("vT", [P, NT, C])
        nmax = sb("nmax", [P, HG, NT])
        nmax_hi = sb("nmax_hi", [P, HG, NT], F32R)
        nmax_parts = sb("nmax_parts", [P, 2, HG, NT])
        shift_rows = sb("shift_rows", [2 * HG * NT, P], F32R)
        biased = sb("biased", [P, S_SLOTS, HALF])
        probs = sb("probs", [P, P_GROUPS * HG, HALF])
        o = sb("o", [P, G, N])
        lnl = sb("lnl", [P, HALF])
        rl = sb("rl", [P, HALF])
        x1 = sb("x1", [P, KC, N])
        hT = sb("hT", [P, NT, C])
        hs = sb("hs", [P, 2, C])
        nmax1 = sb("nmax1", [P, NT])
        l1 = sb("l1", [P, NT])
        rl1 = sb("rl1", [P, NT])

        f_stack = st_q[0:KS, 0, :]
        g_stack = st_k[0:KS, 0, :]
        squares = o
        lnvar = biased[:].rearrange("p (a s) n -> p a (s n)", a=2)[:, 0, :]
        rstd = biased[:].rearrange("p (a s) n -> p a (s n)", a=2)[:, 1, :]
        attn1 = probs[:].rearrange("p (a s) n -> p a (s n)", s=2)
        A1 = P_GROUPS * HG // 2

        wraw = probs[:].rearrange("p s n -> p (s n)")
        wq_raw = wraw[:, 0:6 * C].rearrange("p (t c) -> p t c", c=C)
        wo_raw = wraw[:, 6 * C:8 * C].rearrange("p (t c) -> p t c", c=C)
        wh_raw = wraw[:, 8 * C:10 * C].rearrange("p (t c) -> p t c", c=C)
        wf_raw = wraw[0:C8, 10 * C:11 * C]
        wg_raw = wraw[0:C8, 11 * C:12 * C]
        bh_row = wraw[0:1, 12 * C:13 * C]
        mlp = wraw[0:D0, 13 * C:]
        w0T, w1_raw, w1T = mlp[0:2, 0:D0], mlp[:, D0:2 * D0], mlp[:, 2 * D0:3 * D0]
        w2T, w2_raw = mlp[:, 3 * D0:3 * D0 + G * HG], mlp[0:G * HG, 4 * D0:5 * D0]
        b0_col, b1_col = mlp[:, 5 * D0:5 * D0 + 1], mlp[:, 5 * D0 + 1:5 * D0 + 2]
        b2_col = mlp[0:G * HG, 5 * D0 + 2:5 * D0 + 3]
        w0_raw = mlp[:, 6 * D0:6 * D0 + 2]
        room = bias_lines[:].rearrange("p h n -> p (h n)")
        MSTEPS = 9
        MC = DY * DX // MSTEPS
        assert MC * MSTEPS == DY * DX and MC <= HALF
        rel_sb = room[0:2, 0:DY * DX]
        table_sb = room[0:G * HG, DY * DX:2 * DY * DX]
        h_sum, h_a, h_b = (room[0:D0, 2 * DY * DX + i * MC:2 * DY * DX + (i + 1) * MC] for i in range(3))

        weights_loaded = sem("weights_loaded")
        rel_loaded = sem("rel_loaded")
        table_stored = sem("table_stored")
        lines_stored = sem("lines_stored")
        lines_loaded = sem("lines_loaded")
        ones_set = sem("ones_set")
        w_turned = sem("w_turned")
        w_kept = sem("w_kept")
        mlp_mm = sem("mlp_mm")
        mlp_act = sem("mlp_act")
        mlp_add = sem("mlp_add")
        table_ready = sem("table_ready")
        credit = {}

        def counted(name, per_batch):
            s = sem(name)
            credit[name] = (s, per_batch)
            return s

        x_loaded = counted("x_loaded", 16)
        res_loaded = counted("res_loaded", 16)
        STACK_DMAS = 6 * HG
        stack_loaded = counted("stack_loaded", G * STACK_DMAS * 16)
        rows_loaded = counted("rows_loaded", G * 32)
        y_stored = counted("y_stored", 16)
        mean_mm = counted("mean_mm", 1)
        var_mm = counted("var_mm", 1)
        qk_mm = counted("qk_mm", 2 * G)
        v_mm = counted("v_mm", NT)
        a_mm = counted("a_mm", G * HG * NT)
        shift_mm = counted("shift_mm", G)
        s_mm = counted("s_mm", G * TG * HG)
        pv_mm = counted("pv_mm", G * TG)
        proj_mm = counted("proj_mm", KC * NHALF)
        fg_mm = counted("fg_mm", 2)
        h_mm = counted("h_mm", NT)
        s1_mm = counted("s1_mm", NT)
        sa_mm = counted("sa_mm", NT)
        centered = counted("centered", KC)
        normed = counted("normed", KC)
        lo_ready = counted("lo_ready", 2 * G)
        a_max = counted("a_max", G * HG * NT)
        split_hi = counted("split_hi", G)
        parts_ready = counted("parts_ready", G)
        bias_added = counted("bias_added", G * TG * HG)
        o_ready = counted("o_ready", G * NHALF)
        x1_ready = counted("x1_ready", KC * NHALF)
        fg_lo = counted("fg_lo", 2)
        h_ready = counted("h_ready", NT)
        nmax1_ready = counted("nmax1_ready", NT)
        rl1_ready = counted("rl1_ready", NT)
        hs_ready = counted("hs_ready", NT)
        y_ready = counted("y_ready", KC * NHALF)
        squared = counted("squared", KC)
        rstd_ready = counted("rstd_ready", 2)
        hi_ready = counted("hi_ready", 2 * G)
        v_ready = counted("v_ready", NT)
        rows_ready = counted("rows_ready", G)
        probs_ready = counted("probs_ready", G * TG * HG)
        rl_ready = counted("rl_ready", 2 * G * NHALF)
        fg_hi = counted("fg_hi", 2)
        e1_ready = counted("e1_ready", NT)
        per_batch = {name: k for name, (s, k) in credit.items()}

        SEMS = {name: s for name, (s, k) in credit.items()}

        def need(eng, name, b, n, after=None):
            value = b * per_batch[name] + (per_batch[name] + n)
            if after is None and eng is nc.sync:
                after = (lines_loaded, 16 * ROWS)
            if after is not None:
                value = eng.to_reg(value)
                eng.wait_ge(*after)
            eng.wait_ge(SEMS[name], value)

        block = ctx.enter_context(nc.Block())

        @block.sync
        def _(sp):
            for name in ("x_loaded", "res_loaded", "stack_loaded", "rows_loaded", "y_stored"):
                sp.sem_inc(SEMS[name], per_batch[name])
            n = 0
            for dst, src in (
                (ident[:], ident_in),
                (wq_raw, w_qkv.rearrange("(t p) c -> p t c", p=P)),
                (wo_raw, w_out.rearrange("(t p) c -> p t c", p=P)),
                (wh_raw, Wh.rearrange("(t p) c -> p t c", p=P)),
                (wf_raw, Wf), (wg_raw, Wg),
                (bh_row, bh.rearrange("(a c) -> a c", a=1)),
                (gamma_col[:, 0:1], gamma[0, 0:P].rearrange("p a b -> p (a b)")),
                (gamma_col[:, 1:2], gamma[0, P:2 * P].rearrange("p a b -> p (a b)")),
                (gamma1_col[:], gamma1.rearrange("(a b) -> a b", a=1).broadcast_to((P, 1))),
                (w0_raw, w0), (w1_raw, w1), (w2_raw, w2),
                (b0_col, b0.rearrange("(a b) -> a b", b=1)),
                (b1_col, b1.rearrange("(a b) -> a b", b=1)),
                (b2_col, b2.rearrange("(a b) -> a b", b=1)),
            ):
                sp.dma_start(dst, src).then_inc(weights_loaded, 16)
                n += 1
            for part in range(KS // HD):
                sp.dma_start(bfg[part * HD:(part + 1) * HD, 0:1],
                             bf.rearrange("(a b) -> a b", b=1)).then_inc(weights_loaded, 16)
                sp.dma_start(bfg[part * HD:(part + 1) * HD, 1:2],
                             bg.rearrange("(a b) -> a b", b=1)).then_inc(weights_loaded, 16)
                n += 2
            assert n == N_WEIGHTS
            sp.dma_start(rel_sb, rel_log).then_inc(rel_loaded, 16)
            sp.wait_ge(table_ready, MSTEPS)
            sp.dma_start(table_dram.ap(), table_sb).then_inc(table_stored, 16)
            sp.wait_ge(table_stored, 16)
            for x in range(W):
                src = table_dram.ap().rearrange("h (a w) -> h a w", w=DX)[:, :, W - 1 - x:2 * W - 1 - x]
                sp.dma_start(lines_dram.ap()[x], src).then_inc(lines_stored, 16)
            sp.wait_ge(lines_stored, 16 * W)
            for yl in range(ROWS):
                sp.dma_start(bias_lines[yl * W:(yl + 1) * W],
                             lines_dram.ap()[:, :, ROWS - 1 - yl:ROWS - 1 - yl + NA]
                             .rearrange("x h a w -> x h (a w)")).then_inc(lines_loaded, 16)

            with sp.Fori(0, B) as b:
                need(sp, "v_mm", b, 0)
                need(sp, "qk_mm", b, 0)
                sp.dma_start(xn[:], x_dram[b]).then_inc(x_loaded, 16)
                for g in range(G):
                    need(sp, "lo_ready", b, 2 * g + 2)
                    need(sp, "s_mm", b, g * TG * HG)
                    for h in range(HG):
                        rows = slice(h * HD, (h + 1) * HD)
                        for r, (qpart, kpart) in enumerate(((0, 0), (0, 1), (1, 0))):
                            dst = slice(r * HD, (r + 1) * HD)
                            sp.dma_start(q_stack[dst, h, :].bitcast(F32),
                                         st_q[rows, qpart, :].bitcast(F32)).then_inc(stack_loaded, 16)
                            sp.dma_start(k_stack[dst, h, :].bitcast(F32),
                                         st_k[rows, kpart, :].bitcast(F32)).then_inc(stack_loaded, 16)
                    need(sp, "rows_ready", b, g + 1)
                    for part in range(2):
                        sp.dma_start(q_stack[KS + part:KS + part + 1].bitcast(F32)
                                     .rearrange("p h (t n) -> p (h t) n", n=P),
                                     shift_rows[part * HG * NT:(part + 1) * HG * NT, :].bitcast(F32)).then_inc(rows_loaded, 16)
                need(sp, "y_stored", b, 0)
                sp.dma_start(x1[:], x_dram[b]).then_inc(res_loaded, 16)
                need(sp, "y_ready", b, KC * NHALF)
                sp.dma_start(out_dram[b], x1[:]).then_inc(y_stored, 16)
            sp.wait_ge(y_stored, 16 * (B + 1))

        @block.tensor
        def _(pe):
            for name in ("mean_mm", "var_mm", "qk_mm", "v_mm", "a_mm", "shift_mm", "s_mm", "pv_mm", "proj_mm",
                         "fg_mm", "h_mm", "s1_mm", "sa_mm"):
                pe.sem_inc(SEMS[name], per_batch[name])
            pe.wait_ge(weights_loaded, 16 * N_WEIGHTS)
            pe.wait_ge(ones_set, 1)
            turned = 0
            for src in tiles_to_turn((wq_raw, wo_raw, wh_raw), (wf_raw, wg_raw), (w0_raw, w1_raw, w2_raw)):
                rows, cols = src.shape
                if turned >= 8:
                    pe.wait_ge(w_kept, turned - 7)
                pe.transpose(psum[0:cols, turned % 8, 0:rows], src, ident[0:rows, 0:rows]).then_inc(w_turned, 1)
                turned += 1
            pe.wait_ge(w_kept, turned)
            pe.matmul(psum[:, 7, 0:C], ones[0:1, :], bh_row, start=True, stop=True).then_inc(w_turned, 1)
            pe.wait_ge(rel_loaded, 16)
            for m in range(MSTEPS):
                if m:
                    pe.wait_ge(mlp_act, 2 * m)
                pe.matmul(psum[0:D0, 0, 0:MC], w0T, rel_sb[:, m * MC:(m + 1) * MC], start=True,
                          stop=True).then_inc(mlp_mm, 1)
                pe.wait_ge(mlp_act, 2 * m + 1)
                pe.matmul(psum[0:D0, 1, 0:MC], w1T, h_a, start=True, stop=True).then_inc(mlp_mm, 1)
                pe.wait_ge(mlp_act, 2 * m + 2)
                if m:
                    pe.wait_ge(table_ready, m)
                pe.matmul(psum[0:G * HG, 2, 0:MC], w2T, h_b, start=True, stop=True).then_inc(mlp_mm, 1)
            pe.wait_ge(table_ready, MSTEPS)

            with pe.Fori(0, B) as b:
                need(pe, "x_loaded", b, 16)
                need(pe, "e1_ready", b, 0)
                for half in range(NHALF):
                    for k in range(KC):
                        mm = pe.matmul(psum[:, half, :], mean_w[:], xn[:, k, half * HALF:(half + 1) * HALF],
                                       start=(k == 0), stop=(k == KC - 1))
                mm.then_inc(mean_mm, 1)
                need(pe, "squared", b, KC)
                for half in range(NHALF):
                    for k in range(KC):
                        mm = pe.matmul(psum[:, 2 + half, :], mean_w[:], squares[:, k, half * HALF:(half + 1) * HALF],
                                       start=(k == 0), stop=(k == KC - 1))
                mm.then_inc(var_mm, 1)

                def project_qk(g):
                    for t in range(2):
                        for half in range(NHALF):
                            for k in range(KC):
                                mm = pe.matmul(psum[:, 2 * t + half, :],
                                               wqkvT[:, k, t * C + g * P:t * C + (g + 1) * P],
                                               xn[:, k, half * HALF:(half + 1) * HALF],
                                               start=(k == 0), stop=(k == KC - 1))
                        mm.then_inc(qk_mm, 1)

                need(pe, "normed", b, KC)
                project_qk(0)
                need(pe, "y_ready", b, 0)
                for t in range(NT):
                    if t >= 4:
                        need(pe, "v_ready", b, t - 3)
                    for k in range(KC):
                        mm = pe.matmul(psum[:, 4 + t % 4, 0:C], xn[:, k, t * P:(t + 1) * P], wqkvT[:, k, 2 * C:3 * C],
                                       start=(k == 0), stop=(k == KC - 1))
                    mm.then_inc(v_mm, 1)

                for g in range(G):
                    need(pe, "stack_loaded", b, (g + 1) * STACK_DMAS * 16)
                    if g:
                        need(pe, "bias_added", b, TG * HG)
                    for m in range(HG * NT):
                        h, t = divmod(m, NT)
                        if m >= 2:
                            need(pe, "a_max", b, g * HG * NT + m - 1)
                        for half in range(NHALF):
                            mm = pe.matmul(psum[:, 2 * (m % 2) + half, :],
                                           q_stack[0:KS, h, t * P:(t + 1) * P],
                                           back(k_stack[0:KS, h, :], half * HALF, HALF, N),
                                           start=True, stop=True)
                        mm.then_inc(a_mm, 1)
                    need(pe, "parts_ready", b, g + 1)
                    if g:
                        need(pe, "o_ready", b, NHALF)
                    else:
                        need(pe, "v_ready", b, NT)
                    pe.matmul(psum[0:2 * HG * NT, 4, 0:P], nmax_parts[:].rearrange("p l h t -> p (l h t)"), ident[:],
                              start=True, stop=True).then_inc(shift_mm, 1)
                    if g + 1 < G:
                        need(pe, "a_max", b, HG * NT)
                        project_qk(g + 1)
                        need(pe, "lo_ready", b, 2 * g + 4)

                    need(pe, "a_max", b, (g + 1) * HG * NT)
                    need(pe, "rows_loaded", b, 32 * (g + 1))
                    for q in range(TG + PV_LAG):
                        if q < TG:
                            half, t = divmod(q, NT)
                            for h in range(HG):
                                n = q * HG + h
                                if n >= S_SLOTS:
                                    need(pe, "bias_added", b, g * TG * HG + n - S_SLOTS + 1)
                                pe.matmul(psum[:, n % S_SLOTS, :], k_stack[:, h, t * P:(t + 1) * P],
                                          back(q_stack[:, h, :], half * HALF, HALF, N),
                                          start=True, stop=True).then_inc(s_mm, 1)
                        if q >= PV_LAG:
                            half, t = divmod(q - PV_LAG, NT)
                            need(pe, "probs_ready", b, (g * TG + q - PV_LAG + 1) * HG)
                            if t == 0 and g * NHALF + half >= NHALF:
                                need(pe, "o_ready", b, (g - 1) * NHALF + half + 1)
                            for h in range(HG):
                                pe.matmul(psum[h * HD:(h + 1) * HD, 4 + half, :],
                                          vT[:, t, (g * HG + h) * HD:(g * HG + h + 1) * HD],
                                          probs[:, (q - PV_LAG) % P_GROUPS * HG + h, :],
                                          start=(t == 0), stop=(t == NT - 1))
                            for h in range(HG):
                                mm = pe.matmul(psum[h * HD:(h + 1) * HD, 6 + half, :], ones[:, 0:HD],
                                               probs[:, (q - PV_LAG) % P_GROUPS * HG + h, :],
                                               start=(t == 0), stop=(t == NT - 1))
                            mm.then_inc(pv_mm, 1)

                need(pe, "bias_added", b, G * TG * HG)
                need(pe, "o_ready", b, G * NHALF)
                for c in range(KC):
                    for half in range(NHALF):
                        for g in range(G):
                            mm = pe.matmul(psum[:, 2 * c + half, :], woutT[:, g, c * P:(c + 1) * P],
                                           o[:, g, half * HALF:(half + 1) * HALF],
                                           start=(g == 0), stop=(g == G - 1))
                        mm.then_inc(proj_mm, 1)
                need(pe, "x1_ready", b, KC * NHALF)
                for t in range(2):
                    for half in range(NHALF):
                        for k in range(KC):
                            mm = pe.matmul(psum[0:KS, 4 + 2 * t + half, :], wfgT[:, k, t, :],
                                           x1[:, k, half * HALF:(half + 1) * HALF],
                                           start=(k == 0), stop=(k == KC - 1))
                    mm.then_inc(fg_mm, 1)
                for t in range(NT):
                    if t >= 4:
                        need(pe, "h_ready", b, t - 3)
                    for k in range(KC):
                        mm = pe.matmul(psum[:, t % 4, 0:C], x1[:, k, t * P:(t + 1) * P], whT[:, k, :],
                                       start=(k == 0), stop=(k == KC - 1))
                    mm.then_inc(h_mm, 1)
                need(pe, "fg_lo", b, 2)
                need(pe, "h_ready", b, NT)
                for t in range(NT + 1):
                    if t < NT:
                        if t >= 2:
                            need(pe, "e1_ready", b, t - 1)
                        for half in range(NHALF):
                            mm = pe.matmul(psum[:, 2 * (t % 2) + half, :], f_stack[:, t * P:(t + 1) * P],
                                           g_stack[:, half * HALF:(half + 1) * HALF], start=True, stop=True)
                        mm.then_inc(s1_mm, 1)
                    if t >= 1:
                        need(pe, "hs_ready", b, t)
                        for c in range(KC):
                            for half in range(NHALF):
                                mm = pe.matmul(psum[:, 4 + 2 * c + half, :], hs[:, (t - 1) % 2, c * P:(c + 1) * P],
                                               attn1[:, (t - 1) % A1, half * HALF:(half + 1) * HALF],
                                               start=(t == 1), stop=(t == NT))
                        mm.then_inc(sa_mm, 1)

        @block.scalar
        def _(act):
            for name in ("squared", "rstd_ready", "hi_ready", "v_ready", "rows_ready", "probs_ready", "rl_ready",
                         "fg_hi", "e1_ready"):
                act.sem_inc(SEMS[name], per_batch[name])
            def divisor(g, half, act, b):
                step = g * NHALF + half
                need(act, "pv_mm", b, g * TG + (half + 1) * NT)
                need(act, "o_ready", b, step)
                nc.scalar.activation(lnl[:], psum[:, 6 + half, :], ACT.Ln).then_inc(rl_ready, 1)
                need(act, "rl_ready", b, 2 * step + 1)
                nc.scalar.activation(rl[:], lnl[:], ACT.Exp, scale=-1.0).then_inc(rl_ready, 1)

            with act.Fori(0, B) as b:
                need(act, "proj_mm", b, 0)
                for k in range(KC):
                    need(act, "centered", b, k + 1)
                    nc.scalar.activation(squares[:, k, :], xn[:, k, :], ACT.Square).then_inc(squared, 1)
                need(act, "var_mm", b, 1)
                nc.scalar.activation(lnvar, pair(2), ACT.Ln, bias=eps_col[:, 0:1]).then_inc(rstd_ready, 1)
                need(act, "rstd_ready", b, 1)
                nc.scalar.activation(rstd, lnvar, ACT.Exp, scale=-0.5).then_inc(rstd_ready, 1)

                def stage(g):
                    for t, st in enumerate((st_q[:, :, ::-1], st_k)):
                        need(act, "qk_mm", b, 2 * g + t + 1)
                        need(act, "stack_loaded", b, g * STACK_DMAS * 16)
                        if g == 0:
                            need(act, "s1_mm", b, 0)
                        nc.scalar.activation(st[:, 0, :], pair(2 * t), ACT.Copy,
                                             scale=(SCALE if t == 0 else 1.0)).then_inc(hi_ready, 1)

                stage(0)
                need(act, "pv_mm", b, 0)
                for t in range(NT):
                    need(act, "v_mm", b, t + 1)
                    nc.scalar.copy(vT[:, t, :], psum[:, 4 + t % 4, 0:C]).then_inc(v_ready, 1)
                for g in range(G):
                    need(act, "shift_mm", b, g + 1)
                    need(act, "rows_loaded", b, 32 * g)
                    nc.scalar.copy(shift_rows[:], psum[0:2 * HG * NT, 4, 0:P]).then_inc(rows_ready, 1)
                    if g + 1 < G:
                        stage(g + 1)
                    if g == 0:
                        need(act, "sa_mm", b, 0)
                    for q in range(TG):
                        if q >= P_GROUPS:
                            need(act, "pv_mm", b, g * TG + q - P_GROUPS + 1)
                        elif g:
                            need(act, "pv_mm", b, g * TG)
                        for h in range(HG):
                            n = q * HG + h
                            need(act, "bias_added", b, g * TG * HG + n + 1)
                            nc.scalar.activation(probs[:, q % P_GROUPS * HG + h, :], biased[:, n % S_SLOTS, :],
                                                 ACT.Exp).then_inc(probs_ready, 1)
                        if q == NT - 1 + PV_LAG:
                            divisor(g, 0, act, b)
                    divisor(g, 1, act, b)
                for t, stack in enumerate((f_stack, g_stack)):
                    need(act, "fg_mm", b, t + 1)
                    need(act, "stack_loaded", b, G * STACK_DMAS * 16)
                    nc.scalar.activation(stack, pair(4 + 2 * t)[0:KS], ACT.Identity,
                                         bias=bfg[:, t:t + 1]).then_inc(fg_hi, 1)
                need(act, "pv_mm", b, G * TG)
                for t in range(NT):
                    need(act, "nmax1_ready", b, t + 1)
                    if t >= A1:
                        need(act, "sa_mm", b, t - A1 + 1)
                    nc.scalar.activation(attn1[:, t % A1, :], pair(2 * (t % 2)), ACT.Exp, bias=nmax1[:, t:t + 1],
                                         accum_out=l1[:, t:t + 1]).then_inc(e1_ready, 1)

        @block.vector
        def _(dve):
            for name in ("centered", "normed", "lo_ready", "a_max", "split_hi", "parts_ready", "bias_added",
                         "o_ready", "x1_ready", "fg_lo", "h_ready", "nmax1_ready", "rl1_ready", "hs_ready", "y_ready"):
                dve.sem_inc(SEMS[name], per_batch[name])
            nc.vector.memset(ones[:], 1.0)
            nc.vector.memset(mean_w[:], 1.0 / C)
            nc.vector.memset(k_stack[KS:KS + 2].bitcast(F32), 1.0)
            nc.vector.memset(eps_col[:], EPS).then_inc(ones_set, 1)
            dve.wait_ge(weights_loaded, 16 * N_WEIGHTS)
            turned = 0

            def turned_in(rows, cols):
                nonlocal turned
                turned += 1
                dve.wait_ge(w_turned, turned)
                return psum[0:cols, (turned - 1) % 8, 0:rows]

            for t in range(3 * KC):
                for k in range(KC):
                    nc.vector.tensor_scalar(wqkvT[:, k, t * P:(t + 1) * P], turned_in(P, P), gamma_col[:, k:k + 1],
                                            None, ALU.mult).then_inc(w_kept, 1)
            for dst in (woutT, whT):
                for t in range(KC):
                    for k in range(KC):
                        nc.vector.tensor_copy(dst[:, k, t * P:(t + 1) * P], turned_in(P, P)).then_inc(w_kept, 1)
            for t in range(2):
                for k in range(KC):
                    src = turned_in(C8, P)
                    for part in range(KS // HD):
                        last = nc.vector.tensor_copy(wfgT[:, k, t, part * HD:(part + 1) * HD], src)
                    last.then_inc(w_kept, 1)
            nc.vector.tensor_copy(w0T, turned_in(D0, 2)).then_inc(w_kept, 1)
            nc.vector.tensor_copy(w1T, turned_in(D0, D0)).then_inc(w_kept, 1)
            nc.vector.tensor_copy(w2T, turned_in(G * HG, D0)).then_inc(w_kept, 1)
            dve.wait_ge(w_turned, turned + 1)
            nc.vector.tensor_copy(bh_all[:], psum[:, 7, 0:C])
            added = 0
            for m in range(MSTEPS):
                for layer, (bank, col, dst) in enumerate(((0, b0_col, h_a), (1, b1_col, h_b))):
                    dve.wait_ge(mlp_mm, 3 * m + layer + 1)
                    nc.vector.tensor_scalar(h_sum, psum[0:D0, bank, 0:MC], col, None,
                                            ALU.add).then_inc(mlp_add, 1)
                    added += 1
                    dve.wait_ge(mlp_add, added)
                    nc.vector.scalar_tensor_tensor(dst, h_sum, LEAK, h_sum, ALU.mult,
                                                   ALU.max).then_inc(mlp_act, 1)
                dve.wait_ge(mlp_mm, 3 * m + 3)
                nc.vector.tensor_scalar(table_sb[:, m * MC:(m + 1) * MC], psum[0:G * HG, 2, 0:MC], b2_col, None, ALU.add).then_inc(table_ready, 1)

            def normalise(g, half, dve, b):
                step = g * NHALF + half
                need(dve, "rl_ready", b, 2 * step + 2)
                if step == 0:
                    need(dve, "proj_mm", b, 0)
                nc.vector.tensor_tensor(o[:, g, half * HALF:(half + 1) * HALF], psum[:, 4 + half, :], rl[:],
                                        ALU.mult).then_inc(o_ready, 1)

            with dve.Fori(0, B) as b:
                need(dve, "mean_mm", b, 1)
                for k in range(KC):
                    nc.vector.tensor_tensor(xn[:, k, :], xn[:, k, :], pair(0), ALU.subtract).then_inc(centered, 1)
                need(dve, "rstd_ready", b, 2)
                need(dve, "centered", b, KC)
                for k in range(KC):
                    nc.vector.tensor_tensor(xn[:, k, :], xn[:, k, :], rstd, ALU.mult).then_inc(normed, 1)

                def stage(g):
                    for t, st in enumerate((st_q[:, :, ::-1], st_k)):
                        need(dve, "hi_ready", b, 2 * g + t + 1)
                        nc.vector.scalar_tensor_tensor(st[:, 1, :], pair(2 * t), (SCALE if t == 0 else 1.0),
                                                       st[:, 0, :].bitcast(F32), ALU.mult,
                                                       ALU.subtract).then_inc(lo_ready, 1)

                stage(0)
                for g in range(G):
                    for m in range(HG * NT):
                        h, t = divmod(m, NT)
                        need(dve, "a_mm", b, g * HG * NT + m + 1, (lines_loaded, 16 * ROWS))
                        a0 = (H - ROWS - ROWS * t) * W
                        nc.vector.tensor_tensor_reduce(pair(2 * (m % 2)), pair(2 * (m % 2)), bias_lines[:, g * HG + h, a0:a0 + N],
                                                       -1.0, BIG, ALU.add, ALU.min,
                                                       nmax[:, h, t:t + 1]).then_inc(a_max, 1)
                    need(dve, "a_max", b, (g + 1) * HG * NT)
                    need(dve, "shift_mm", b, g)
                    nc.vector.tensor_copy(nmax_hi[:], nmax[:]).then_inc(split_hi, 1)
                    need(dve, "split_hi", b, g + 1)
                    nc.vector.tensor_copy(nmax_parts[:, 0], nmax_hi[:].bitcast(F32))
                    nc.vector.tensor_tensor(nmax_parts[:, 1], nmax[:], nmax_hi[:].bitcast(F32),
                                            ALU.subtract).then_inc(parts_ready, 1)
                    if g + 1 < G:
                        stage(g + 1)
                    for q in range(TG):
                        half, t = divmod(q, NT)
                        a0 = (half * (H // NHALF) - ROWS * t + H - ROWS) * W
                        for h in range(HG):
                            n = q * HG + h
                            need(dve, "s_mm", b, g * TG * HG + n + 1)
                            if n >= S_SLOTS:
                                need(dve, "probs_ready", b, g * TG * HG + n - S_SLOTS + 1)
                            elif g:
                                need(dve, "probs_ready", b, g * TG * HG)
                            nc.vector.tensor_tensor(biased[:, n % S_SLOTS, :], psum[:, n % S_SLOTS, :],
                                                    bias_lines[:, g * HG + h, a0:a0 + HALF],
                                                    ALU.add).then_inc(bias_added, 1)
                        if q == NT + PV_LAG + 1:
                            normalise(g, 0, dve, b)
                    normalise(g, 1, dve, b)
                need(dve, "res_loaded", b, 16)
                for c in range(KC):
                    for half in range(NHALF):
                        cols = slice(half * HALF, (half + 1) * HALF)
                        need(dve, "proj_mm", b, c * NHALF + half + 1)
                        nc.vector.tensor_tensor(x1[:, c, cols], x1[:, c, cols], psum[:, 2 * c + half, :],
                                                ALU.add).then_inc(x1_ready, 1)
                for t, (stack, lo) in enumerate(((f_stack, 2), (g_stack, 1))):
                    rows = slice(lo * HD, (lo + 1) * HD)
                    need(dve, "fg_hi", b, t + 1)
                    nc.vector.scalar_tensor_tensor(stack[rows], pair(4 + 2 * t)[rows], bfg[rows, t:t + 1],
                                                   stack[rows].bitcast(F32), ALU.add,
                                                   ALU.subtract).then_inc(fg_lo, 1)
                for t in range(NT):
                    need(dve, "h_mm", b, t + 1)
                    nc.vector.tensor_tensor(hT[:, t, :], psum[:, t % 4, 0:C], bh_all[:], ALU.add).then_inc(h_ready, 1)
                for t in range(NT + 1):
                    if t < NT:
                        need(dve, "s1_mm", b, t + 1)
                        nc.vector.tensor_reduce(nmax1[:, t:t + 1], pair(2 * (t % 2)), AX_X, ALU.max,
                                                negate=True).then_inc(nmax1_ready, 1)
                    if t >= 1:
                        need(dve, "e1_ready", b, t)
                        nc.vector.reciprocal(rl1[:, t - 1:t], l1[:, t - 1:t]).then_inc(rl1_ready, 1)
                        need(dve, "rl1_ready", b, t)
                        need(dve, "h_ready", b, t)
                        if t >= 3:
                            need(dve, "sa_mm", b, t - 2)
                        else:
                            need(dve, "sa_mm", b, 0)
                        nc.vector.tensor_scalar(hs[:, (t - 1) % 2, :], hT[:, t - 1, :], rl1[:, t - 1:t], None,
                                                ALU.mult).then_inc(hs_ready, 1)
                need(dve, "sa_mm", b, NT)
                for c in range(KC):
                    for half in range(NHALF):
                        cols = slice(half * HALF, (half + 1) * HALF)
                        nc.vector.scalar_tensor_tensor(x1[:, c, cols], psum[:, 4 + 2 * c + half, :], gamma1_col[:, 0:1],
                                                       x1[:, c, cols], ALU.mult, ALU.add).then_inc(y_ready, 1)


N_WEIGHTS = 16 + 6


def back(ap, start, count, total):
    first = total - 1 - start
    stop = first - count
    return ap[:, first:(stop if stop >= 0 else None):-1]


def tiles_to_turn(square, narrow, small):
    for raw in square:
        for t in range(raw.shape[1]):
            for k in range(raw.shape[2] // P):
                yield raw[:, t, k * P:(k + 1) * P]
    for raw in narrow:
        for k in range(raw.shape[1] // P):
            yield raw[:, k * P:(k + 1) * P]
    yield from small


_INS = ["x", "L0_conv_gamma", "L0_conv_w_qkv", "L0_conv_w_out", "L0_conv_cpb_w0", "L0_conv_cpb_b0",
        "L0_conv_cpb_w1", "L0_conv_cpb_b1", "L0_conv_cpb_w2", "L0_conv_cpb_b2", "L1_conv_Wf", "L1_conv_bf",
        "L1_conv_Wg", "L1_conv_bg", "L1_conv_Wh", "L1_conv_bh", "L1_conv_gamma"]
_OUTS = [((8, 256, 32, 32), "float32")]


def shape_constants(side):
    d = np.arange(1 - side, side, dtype=np.float32)
    line = (np.sign(d) * np.log(np.abs(d) + np.float32(1.0))).astype(np.float32)
    dy, dx = np.meshgrid(line, line, indexing="ij")
    return [np.stack([dy.ravel(), dx.ravel()]), np.eye(P, dtype=np.float32)]


def kernel(**inputs):
    import concourse.bacc as bacc
    from concourse.bass_utils import run_bass_kernel_spmd

    nc = bacc.Bacc("TRN2", target_bir_lowering=False, num_devices=1)
    arrays, args = {}, []
    named = [(n, np.ascontiguousarray(inputs[n])) for n in _INS]
    named += list(zip(("rel_log", "identity"), shape_constants(inputs["x"].shape[2])))
    for name, a in named:
        arrays[f"in_{name}_dram"] = a
        args.append(nc.dram_tensor(f"in_{name}_dram", a.shape, mybir.dt.from_np(a.dtype), kind="ExternalInput").ap())
    for i, (shape, dtype) in enumerate(_OUTS):
        args.append(nc.dram_tensor(f"out_{i}_dram", shape, mybir.dt.from_np(np.dtype(dtype)),
                                   kind="ExternalOutput").ap())
    two_layer_attention(nc, *args)
    r = run_bass_kernel_spmd(nc, [arrays], core_ids=[0])
    return r.results[0]["out_0_dram"]
```

```python
from contextlib import ExitStack

import numpy as np

import concourse.bass as bass
from concourse import mybir

ALU = mybir.AluOpType
ACT = mybir.ActivationFunctionType
AX_X = mybir.AxisListType.X
F32 = mybir.dt.float32
F32R = mybir.dt.float32r

P = 128
HD = 32
HG = P // HD
EPS = 1e-5
LEAK = 0.1
BIG = 3.0e38
HP = HG // 2
P_SLOTS = 5
PV_LAG = 1


def two_layer_attention(nc, x, gamma, w_qkv, w_out, w0, b0, w1, b1, w2, b2,
                        Wf, bf, Wg, bg, Wh, bh, gamma1, rel_log, ident_in, out):
    B, C, H, W = x.shape
    N = H * W
    KC = C // P
    NT = N // P
    HALF = 512
    NHALF = N // HALF
    G = C // P
    ROWS = P // W
    DY, DX = 2 * H - 1, 2 * W - 1
    NA = H + (NT - 1) * ROWS
    D0 = w0.shape[0]
    SCALE = HD ** -0.5
    C8 = Wf.shape[0]
    KS = 3 * HD
    TG = NHALF * NT

    x_dram = x.rearrange("b (k p) h w -> b p k (h w)", p=P)
    out_dram = out.rearrange("b (k p) h w -> b p k (h w)", p=P)
    table_dram = nc.dram_tensor("bias_table", [G * HG, DY * DX], F32)
    q_dram = nc.dram_tensor("q_parts", [2, HG, HD, N], F32)
    k_dram = nc.dram_tensor("k_parts", [2, HG, HD, N], F32)
    lines_dram = nc.dram_tensor("bias_lines", [W, G * HG, DY, W], F32)

    with ExitStack() as ctx:
        def sb(name, shape, dt=F32):
            return ctx.enter_context(nc.sbuf_tensor(name, shape, dt))

        def sem(name):
            return ctx.enter_context(nc.semaphore(name))

        psum = ctx.enter_context(nc.psum_tensor("psum", [P, 8, HALF], F32))

        def pair(bank):
            return psum[:, bank:bank + 2, :].rearrange("p a b -> p (a b)")

        ident = sb("ident", [P, P])
        mean_w = sb("mean_w", [P, P])
        eps_col = sb("eps_col", [P, 1])
        wqkvT = sb("wqkvT", [P, KC, 3 * C])
        woutT = sb("woutT", [P, G, C])
        whT = sb("whT", [P, KC, C])
        wfgT = sb("wfgT", [P, KC, 2, KS])
        bfg = sb("bfg", [KS, 2])
        bh_all = sb("bh_all", [P, C])
        gamma_col = sb("gamma_col", [P, KC])
        gamma1_col = sb("gamma1_col", [P, 1])
        bias_lines = sb("bias_lines_sb", [P, G * HG, NA * W])
        xn = sb("xn", [P, KC, N])
        st = sb("st", [P, 2, N], F32R)
        q_stack = sb("q_stack", [KS + 2, G, HG, N], F32R)
        k_stack = sb("k_stack", [KS + 2, HG, N], F32R)
        vT = sb("vT", [P, NT, C])
        nmax = sb("nmax", [P, HG * NT])
        rowsum = sb("rowsum", [P, HG * NT])
        lnsum = sb("lnsum", [P, HG * NT])
        invsum = sb("invsum", [P, HG * NT])
        shift = sb("shift", [P, 3, HG * NT])
        shift_hi = sb("shift_hi", [P, HG * NT], F32R)
        shift_parts = sb("shift_parts", [P, 2, HG * NT])
        shift_rows = sb("shift_rows", [2 * HG * NT, P], F32R)
        biased = sb("biased", [P, 2, N])
        probs = sb("probs", [P, P_SLOTS, 2, HALF])
        o = sb("o", [P, G, N])
        x1 = sb("x1", [P, KC, N])
        fg_stack = sb("fg_stack", [KS, 2, N], F32R)
        nmax1 = sb("nmax1", [P, NT])
        l1 = sb("l1", [P, NT])
        rl1 = sb("rl1", [P, NT])

        squares = st[:].bitcast(F32)
        lnvar = o[:, 1, :]
        rstd = o[:, 1, :]
        attn1 = probs[:, 0:2].rearrange("p s h n -> p s (h n)")
        hT = probs[:, 2:4].rearrange("p s h n -> p (s h n)").rearrange("p (t c) -> p t c", c=C)
        hs = probs[:, 4, 0].rearrange("p (s c) -> p s c", c=C)

        wraw = probs[:].rearrange("p s h n -> p (s h n)")
        wq_raw = wraw[:, 0:6 * C].rearrange("p (t c) -> p t c", c=C)
        wo_raw = wraw[:, 6 * C:8 * C].rearrange("p (t c) -> p t c", c=C)
        wh_raw = wraw[:, 8 * C:10 * C].rearrange("p (t c) -> p t c", c=C)
        wf_raw = wraw[0:C8, 10 * C:11 * C]
        wg_raw = wraw[0:C8, 11 * C:12 * C]
        mlp = wraw[0:D0, 12 * C:]
        w0T, w1_raw, w1T = mlp[0:2, 0:D0], mlp[:, D0:2 * D0], mlp[:, 2 * D0:3 * D0]
        w2T, w2_raw = mlp[:, 3 * D0:3 * D0 + G * HG], mlp[0:G * HG, 4 * D0:5 * D0]
        b0_col, b1_col = mlp[:, 5 * D0:5 * D0 + 1], mlp[:, 5 * D0 + 1:5 * D0 + 2]
        b2_col = mlp[0:G * HG, 5 * D0 + 2:5 * D0 + 3]
        w0_raw = mlp[:, 6 * D0:6 * D0 + 2]
        room = bias_lines[:].rearrange("p h n -> p (h n)")
        MSTEPS = 9
        MC = DY * DX // MSTEPS
        assert MC * MSTEPS == DY * DX and MC <= HALF
        rel_sb = room[0:2, 0:DY * DX]
        table_sb = room[0:G * HG, DY * DX:2 * DY * DX]
        h_sum, h_a, h_b = (room[0:D0, 2 * DY * DX + i * MC:2 * DY * DX + (i + 1) * MC] for i in range(3))

        weights_loaded = sem("weights_loaded")
        rel_loaded = sem("rel_loaded")
        table_stored = sem("table_stored")
        lines_stored = sem("lines_stored")
        consts_set = sem("consts_set")
        w_turned = sem("w_turned")
        w_kept = sem("w_kept")
        mlp_mm = sem("mlp_mm")
        mlp_act = sem("mlp_act")
        mlp_add = sem("mlp_add")
        table_ready = sem("table_ready")
        credit = {}

        def counted(name, per_batch):
            s = sem(name)
            credit[name] = (s, per_batch)
            return s

        x_loaded = counted("x_loaded", 16)
        res_loaded = counted("res_loaded", 16)
        Q_DMAS = 3 * 16
        K_DMAS = 2 * 3 * 16
        q_stored = counted("q_stored", G * 16)
        q_loaded = counted("q_loaded", G * Q_DMAS)
        k_stored = counted("k_stored", G * 16)
        k_loaded = counted("k_loaded", G * K_DMAS)
        rows_loaded = counted("rows_loaded", G * 32)
        y_stored = counted("y_stored", 16)
        TENSOR = dict(mean_mm=1, var_mm=1, qk_mm=2 * G, v_mm=NT, a_mm=G * HG * NT, shift_mm=G, s_mm=G * TG * HP,
                      pv_mm=G * TG, proj_mm=KC * NHALF, fg_mm=2, h_mm=NT, s1_mm=NT, sa_mm=NT)
        VECTOR = dict(centered=KC, normed=KC, lo_ready=2 * G, a_max=G * HG * NT, scaled=G, shifted=2 * G, split_hi=G,
                      parts_ready=G, bias_added=G * TG * HP, x1_ready=KC * NHALF, fg_lo=2, h_ready=NT,
                      nmax1_ready=NT, rl1_ready=NT, hs_ready=NT, y_ready=KC * NHALF)
        SCALAR = dict(squared=KC, rstd_ready=2, hi_ready=2 * G, v_ready=NT, sum_ready=G * HG * NT, ln_ready=2 * G,
                      rows_ready=G, probs_ready=G * TG * HP, o_ready=G * NHALF, fg_hi=2, e1_ready=NT)
        for kind in (TENSOR, VECTOR, SCALAR):
            for name, n in kind.items():
                counted(name, n)
        lines_loaded = sem("lines_loaded")
        per_batch = {name: k for name, (s, k) in credit.items()}

        SEMS = {name: s for name, (s, k) in credit.items()}

        def need(eng, name, b, n):
            value = b * per_batch[name] + (per_batch[name] + n)
            if isinstance(value, int):
                if value > 0:
                    eng.wait_ge(SEMS[name], value)
            elif eng is nc.sync:
                need_beside(eng, (lines_stored, 16 * W), (name, b, n))
            else:
                eng.wait_ge(SEMS[name], value)

        def need_beside(eng, constant, *waits):
            values = [(name, b * per_batch[name] + (per_batch[name] + n)) for name, b, n in waits]
            values = [(name, v if isinstance(v, int) else eng.to_reg(v)) for name, v in values]
            eng.wait_ge(*constant)
            for name, v in values:
                eng.wait_ge(SEMS[name], v)

        A_TILES = HG * NT
        TAIL = A_TILES
        side_0 = [(t, "v", t) for t in range(NT)]
        side_0 += [(NT, "q", 0), (NT + 1, "q", 1), (NT + 2, "split_q", 0), (NT + 2, "k", 0), (NT + 3, "k", 1)]
        side_0 += [(12 + 2 * j, "proj", j) for j in range(KC * NHALF)]
        side_0 += [(13 + 2 * j, "add_x", j) for j in range(KC * NHALF)]
        side_0 += [(18, "split_k", 0), (20, "f", 0), (21, "f", 1), (22, "split_f", 0)]
        side_0 += [(25, "g", 0), (26, "g", 1), (27, "split_g", 0)]
        side_1 = [(0, "mean", 0), (1, "centre", 0), (2, "square", 0), (3, "var", 0), (4, "rstd", 0), (5, "norm", 0)]
        side_1 += [(7, "q", 0), (8, "q", 1), (9, "split_q", 0), (9, "k", 0), (10, "k", 1)]
        side_1 += [(11 + t // 2, "h", t) for t in range(NT)]
        side_1 += [(11 + (t + 1) // 2, "keep_h", t) for t in range(NT)]
        side_1 += [(15, "split_k", 0)]
        for t in range(NT):
            side_1 += [(16 + 2 * t, "s1", t), (16 + 2 * t, "max1", t), (17 + 2 * t, "scale_h", t),
                       (18 + 2 * t, "sa", 2 * t), (19 + 2 * t if t + 1 < NT else TAIL, "sa", 2 * t + 1)]
        side_1 += [(TAIL, "add_y", 0)]
        LAYER_1 = ("proj", "add_x", "f", "split_f", "g", "split_g", "h", "keep_h", "s1", "max1", "scale_h", "sa",
                   "add_y")
        AHEAD = ("mean", "centre", "square", "var", "rstd", "norm")
        QK = ("q", "k", "split_q", "split_k")

        def side_work(g, b, m, first, last, at_once=False):
            for at, kind, arg in (side_0, side_1)[g]:
                if at != m:
                    continue
                if kind in LAYER_1:
                    if not first:
                        yield kind, arg, b - 1
                elif kind in AHEAD or (kind in QK and g == 1):
                    if not last:
                        yield kind, arg, b + 1
                else:
                    yield kind, arg, b

        def ring(g, first):
            items = []
            for m in range(A_TILES):
                items.append(("a", m))
                if g == 1 and not first:
                    items += [("s1", arg) for at, kind, arg in side_1 if at == m and kind == "s1"]
            return items

        def slot_of(g, first, item):
            return ring(g, first).index(item) % 2

        def before_in_slot(g, first, item):
            items = ring(g, first)
            n = items.index(item)
            return items[n - 2] if n >= 2 else None

        def alone(kinds):
            for schedule in (side_0, side_1):
                for at, kind, arg in sorted(schedule, key=lambda entry: entry[0]):
                    if kind in kinds:
                        yield kind, arg, B - 1

        def batches(eng, body):
            body(0, first=True, last=False)
            with eng.Fori(1, B - 1) as b:
                body(b, first=False, last=False)
            body(B - 1, first=False, last=True)

        PAIR_BANKS = (0, 2, 6)
        S_SLOTS = len(PAIR_BANKS)
        SN = TG * HP
        KCHUNKS = (0, 3 * NT // 4 * P, N)

        block = ctx.enter_context(nc.Block())

        @block.sync
        def _(sp):
            for name in ("x_loaded", "res_loaded", "q_stored", "q_loaded", "k_stored", "k_loaded", "rows_loaded",
                         "y_stored"):
                sp.sem_inc(SEMS[name], per_batch[name])
            sp.dma_start(xn[:], x_dram[0]).then_inc(x_loaded, 16)
            n = 0
            for dst, src in (
                (ident[:], ident_in),
                (wq_raw, w_qkv.rearrange("(t p) c -> p t c", p=P)),
                (wo_raw, w_out.rearrange("(t p) c -> p t c", p=P)),
                (wh_raw, Wh.rearrange("(t p) c -> p t c", p=P)),
                (wf_raw, Wf), (wg_raw, Wg),
                (bh_all[:], bh.rearrange("(a c) -> a c", a=1).broadcast_to((P, C))),
                (gamma_col[:, 0:1], gamma[0, 0:P].rearrange("p a b -> p (a b)")),
                (gamma_col[:, 1:2], gamma[0, P:2 * P].rearrange("p a b -> p (a b)")),
                (gamma1_col[:], gamma1.rearrange("(a b) -> a b", a=1).broadcast_to((P, 1))),
                (w0_raw, w0), (w1_raw, w1), (w2_raw, w2),
                (b0_col, b0.rearrange("(a b) -> a b", b=1)),
                (b1_col, b1.rearrange("(a b) -> a b", b=1)),
                (b2_col, b2.rearrange("(a b) -> a b", b=1)),
            ):
                sp.dma_start(dst, src).then_inc(weights_loaded, 16)
                n += 1
            for part in range(KS // HD):
                sp.dma_start(bfg[part * HD:(part + 1) * HD, 0:1],
                             bf.rearrange("(a b) -> a b", b=1)).then_inc(weights_loaded, 16)
                sp.dma_start(bfg[part * HD:(part + 1) * HD, 1:2],
                             bg.rearrange("(a b) -> a b", b=1)).then_inc(weights_loaded, 16)
                n += 2
            assert n == N_WEIGHTS
            sp.dma_start(rel_sb, rel_log).then_inc(rel_loaded, 16)
            sp.wait_ge(table_ready, MSTEPS)
            sp.dma_start(table_dram.ap(), table_sb).then_inc(table_stored, 16)
            sp.wait_ge(table_stored, 16)
            for x in range(W):
                src = table_dram.ap().rearrange("h (a w) -> h a w", w=DX)[:, :, W - 1 - x:2 * W - 1 - x]
                sp.dma_start(lines_dram.ap()[x], src).then_inc(lines_stored, 16)
            sp.wait_ge(lines_stored, 16 * W)
            for yl in range(ROWS):
                sp.dma_start(bias_lines[yl * W:(yl + 1) * W],
                             lines_dram.ap()[:, :, ROWS - 1 - yl:ROWS - 1 - yl + NA]
                             .rearrange("x h a w -> x h (a w)")).then_inc(lines_loaded, 16)


            def through_dram(dram, store_sem):
                sp.dma_start(dram.ap().rearrange("l h d n -> (h d) l n"), st[:].bitcast(F32)).then_inc(store_sem, 16)

            def q_rows(b, g, stacks_done):
                need(sp, "lo_ready", b, 2 * g + 1)
                need(sp, "q_loaded", b, g * Q_DMAS)
                through_dram(q_dram, q_stored)
                need(sp, "q_stored", b, 16 * (g + 1))
                need(sp, *stacks_done)
                for r, part in enumerate((0, 0, 1)):
                    sp.dma_start(q_stack[r * HD:(r + 1) * HD, g].bitcast(F32),
                                 q_dram.ap()[part].rearrange("h d n -> d h n")).then_inc(q_loaded, 16)

            def k_out(b, g):
                need(sp, "lo_ready", b, 2 * g + 2)
                need(sp, "k_loaded", b, g * K_DMAS)
                through_dram(k_dram, k_stored)

            def k_in(b, g, chunk):
                need(sp, "k_stored", b, 16 * (g + 1))
                cols = slice(KCHUNKS[chunk], KCHUNKS[chunk + 1])
                for r, part in enumerate((0, 1, 0)):
                    sp.dma_start(k_stack[r * HD:(r + 1) * HD, :, cols].bitcast(F32),
                                 k_dram.ap()[part, :, :, cols].rearrange("h d n -> d h n")).then_inc(k_loaded, 16)

            def shift_to_stack(b, g):
                need(sp, "rows_ready", b, g + 1)
                for part in range(2):
                    sp.dma_start(q_stack[KS + part:KS + part + 1, g].bitcast(F32)
                                 .rearrange("p h (t n) -> p (h t) n", n=P),
                                 shift_rows[part * HG * NT:(part + 1) * HG * NT, :]
                                 .bitcast(F32)).then_inc(rows_loaded, 16)

            def residual_in(b):
                need(sp, "y_stored", b, 0)
                sp.dma_start(x1[:], x_dram[b]).then_inc(res_loaded, 16)

            def result_out(b):
                need(sp, "y_ready", b, KC * NHALF)
                sp.dma_start(out_dram[b], x1[:]).then_inc(y_stored, 16)

            q_rows(0, 0, ("s_mm", -1, SN))
            k_out(0, 0)
            k_in(0, 0, 0)
            k_in(0, 0, 1)

            def element(b, first, last):
                if not first:
                    residual_in(b - 1)
                q_rows(b, 1, ("s_mm", b, 0))
                if not last:
                    need(sp, "v_mm", b, NT)
                    need(sp, "qk_mm", b, 2 * G)
                    sp.dma_start(xn[:], x_dram[b + 1]).then_inc(x_loaded, 16)
                k_out(b, 1)
                shift_to_stack(b, 0)
                for chunk in range(2):
                    need(sp, "s_mm", b, KCHUNKS[chunk + 1] // P * NHALF * HP)
                    k_in(b, 1, chunk)
                if not last:
                    q_rows(b + 1, 0, ("s_mm", b, SN))
                    k_out(b + 1, 0)
                shift_to_stack(b, 1)
                if not first:
                    result_out(b - 1)
                if not last:
                    for chunk in range(2):
                        need(sp, "s_mm", b, SN + KCHUNKS[chunk + 1] // P * NHALF * HP)
                        k_in(b + 1, 0, chunk)

            batches(sp, element)
            residual_in(B - 1)
            result_out(B - 1)
            sp.wait_ge(y_stored, 16 * (B + 1))

        @block.tensor
        def _(pe):
            for name in TENSOR:
                pe.sem_inc(SEMS[name], per_batch[name])
            pe.wait_ge(weights_loaded, 16 * N_WEIGHTS)
            pe.wait_ge(consts_set, 1)
            turned = 0
            for src in tiles_to_turn((wq_raw, wo_raw, wh_raw), (wf_raw, wg_raw), (w0_raw, w1_raw, w2_raw)):
                rows, cols = src.shape
                if turned >= 8:
                    pe.wait_ge(w_kept, turned - 7)
                pe.transpose(psum[0:cols, turned % 8, 0:rows], src, ident[0:rows, 0:rows]).then_inc(w_turned, 1)
                turned += 1
            pe.wait_ge(w_kept, turned)
            pe.wait_ge(rel_loaded, 16)
            for m in range(MSTEPS):
                if m:
                    pe.wait_ge(mlp_act, 2 * m)
                pe.matmul(psum[0:D0, 0, 0:MC], w0T, rel_sb[:, m * MC:(m + 1) * MC], start=True,
                          stop=True).then_inc(mlp_mm, 1)
                pe.wait_ge(mlp_act, 2 * m + 1)
                pe.matmul(psum[0:D0, 1, 0:MC], w1T, h_a, start=True, stop=True).then_inc(mlp_mm, 1)
                pe.wait_ge(mlp_act, 2 * m + 2)
                if m:
                    pe.wait_ge(table_ready, m)
                pe.matmul(psum[0:G * HG, 2, 0:MC], w2T, h_b, start=True, stop=True).then_inc(mlp_mm, 1)
            pe.wait_ge(table_ready, MSTEPS)

            def halves(b, stage, arg, first_bank, lhsT, rhs, done):
                for k in range(KC):
                    mm = pe.matmul(psum[:, first_bank + arg, :] if stage != "fg" else psum[0:KS, first_bank + arg, :],
                                   lhsT(k), rhs(k), start=(k == 0), stop=(k == KC - 1))
                if done:
                    mm.then_inc(SEMS[done], 1)

            def tokens(src, arg):
                return lambda k: src[:, k, arg * HALF:(arg + 1) * HALF]

            def do(kind, arg, b, g, first, last, tail=False):
                if kind == "mean":
                    need(pe, "x_loaded", b, 16)
                    need(pe, "o_ready", b - 1, NHALF)
                    for half in range(NHALF):
                        halves(b, kind, half, 4, lambda k: mean_w[:], tokens(xn, half), None if half == 0 else "mean_mm")
                elif kind == "var":
                    need(pe, "squared", b, KC)
                    need(pe, "bias_added", b - 1, SN)
                    for half in range(NHALF):
                        halves(b, kind, half, 6, lambda k: mean_w[:], tokens(squares, half),
                               None if half == 0 else "var_mm")
                elif kind == "q":
                    need(pe, "normed", b, KC)
                    if g == 0:
                        need(pe, "v_ready", b, 6)
                    ng = 1 - g
                    halves(b, kind, arg, 4, lambda k: wqkvT[:, k, ng * P:(ng + 1) * P], tokens(xn, arg),
                           "qk_mm" if arg else None)
                elif kind == "k":
                    if g == 0:
                        need(pe, "v_ready", b, NT)
                    ng = 1 - g
                    halves(b, kind, arg, 6, lambda k: wqkvT[:, k, C + ng * P:C + (ng + 1) * P], tokens(xn, arg),
                           "qk_mm" if arg else None)
                elif kind == "v":
                    if arg < 4:
                        need(pe, "o_ready", b, 0)
                        need(pe, "bias_added", b, 0)
                    else:
                        need(pe, "v_ready", b, arg - 3)
                    for k in range(KC):
                        mm = pe.matmul(psum[:, 4 + arg % 4, 0:C], xn[:, k, arg * P:(arg + 1) * P],
                                       wqkvT[:, k, 2 * C:3 * C], start=(k == 0), stop=(k == KC - 1))
                    mm.then_inc(SEMS["v_mm"], 1)
                elif kind == "proj":
                    if arg == 0:
                        need(pe, "o_ready", b, G * NHALF)
                        if not tail:
                            need(pe, "lo_ready", b + 1, 3)
                    elif arg >= 2:
                        need(pe, "x1_ready", b, arg - 1)
                    c, half = divmod(arg, NHALF)
                    halves(b, kind, arg % 2, 4, lambda gg: woutT[:, gg, c * P:(c + 1) * P], tokens(o, half), "proj_mm")
                elif kind in ("f", "g"):
                    t = ("f", "g").index(kind)
                    if arg == 0:
                        need(pe, "x1_ready", b, KC * NHALF)
                        if t:
                            need(pe, "fg_lo", b, 1)
                    halves(b, "fg", arg, 4, lambda k: wfgT[:, k, t, :], tokens(x1, arg), "fg_mm" if arg else None)
                elif kind == "h":
                    if arg >= 2:
                        need(pe, "h_ready", b, arg - 1)
                    elif tail:
                        need(pe, "fg_lo", b, 2)
                    elif last:
                        need(pe, "o_ready", b + 1, NHALF)
                    else:
                        need(pe, "lo_ready", b + 2, 1)
                    for k in range(KC):
                        mm = pe.matmul(psum[:, 4 + arg % 2, 0:C], x1[:, k, arg * P:(arg + 1) * P], whT[:, k, :],
                                       start=(k == 0), stop=(k == KC - 1))
                    mm.then_inc(SEMS["h_mm"], 1)
                elif kind == "s1":
                    if arg == 0:
                        need(pe, "fg_lo", b, 2)
                    slot = slot_free(("s1", arg), b + 1, g, first, tail)
                    for half in range(NHALF):
                        mm = pe.matmul(psum[:, 2 * slot + half, :], fg_stack[:, 0, arg * P:(arg + 1) * P],
                                       fg_stack[:, 1, half * HALF:(half + 1) * HALF], start=True, stop=True)
                    mm.then_inc(SEMS["s1_mm"], 1)
                elif kind == "sa":
                    t, c = divmod(arg, KC)
                    if arg == 0:
                        need(pe, "h_ready", b, NT)
                        if tail or last:
                            need(pe, "bias_added", b + 1, SN if last else 0)
                        else:
                            need(pe, "lo_ready", b + 2, 2)
                    need(pe, "hs_ready", b, t + 1)
                    for half in range(NHALF):
                        mm = pe.matmul(psum[:, 4 + 2 * c + half, :], hs[:, t % 2, c * P:(c + 1) * P],
                                       attn1[:, t % 2, half * HALF:(half + 1) * HALF],
                                       start=(t == 0), stop=(t == NT - 1))
                    if c == KC - 1:
                        mm.then_inc(SEMS["sa_mm"], 1)

            def slot_free(item, b, g, first, tail=False):
                if tail:
                    if item[1] < 2:
                        need(pe, "bias_added", B - 1, G * SN)
                    else:
                        need(pe, "e1_ready", B - 1, item[1] - 1)
                    return item[1] % 2
                prior = before_in_slot(g, first, item)
                if prior is None:
                    need(pe, "bias_added", b, g * SN)
                elif prior[0] == "a":
                    need(pe, "a_max", b, g * A_TILES + prior[1] + 1)
                else:
                    need(pe, "e1_ready", b - 1, prior[1] + 1)
                return slot_of(g, first, item)

            def rows_phase(b, g, first, last):
                need(pe, "q_loaded", b, (g + 1) * Q_DMAS)
                need(pe, "k_loaded", b, (g + 1) * K_DMAS)
                for m in range(A_TILES):
                    h, t = divmod(m, NT)
                    slot = slot_free(("a", m), b, g, first)
                    for half in range(NHALF):
                        mm = pe.matmul(psum[:, 2 * slot + half, :], q_stack[0:KS, g, h, t * P:(t + 1) * P],
                                       back(k_stack[0:KS, h, :], half * HALF, HALF, N), start=True, stop=True)
                    mm.then_inc(SEMS["a_mm"], 1)
                    for kind, arg, e in side_work(g, b, m, first, last):
                        do(kind, arg, e, g, first, last)
                for kind, arg, e in side_work(g, b, TAIL, first, last):
                    do(kind, arg, e, g, first, last)
                need(pe, "parts_ready", b, g + 1)
                if g == 1 and not first:
                    need(pe, "e1_ready", b - 1, NT)
                pe.matmul(psum[0:2 * HG * NT, 0, 0:P], shift_parts[:].rearrange("p l m -> p (l m)"), ident[:],
                          start=True, stop=True).then_inc(SEMS["shift_mm"], 1)

            def columns_phase(b, g, first, last):
                for q in range(TG + PV_LAG):
                    if q < TG:
                        t, half = divmod(q, NHALF)
                        for j in range(HP):
                            n = q * HP + j
                            if n == 0:
                                need(pe, "rows_ready", b, g + 1)
                                need(pe, "rows_loaded", b, 32 * (g + 1))
                            elif n == 2:
                                if g == 0:
                                    need(pe, "lo_ready", b, 4)
                                else:
                                    if not last:
                                        need(pe, "lo_ready", b + 1, 2)
                                    if not first:
                                        need(pe, "y_ready", b - 1, KC * NHALF)
                            elif n >= S_SLOTS:
                                need(pe, "bias_added", b, g * SN + n - S_SLOTS + 1)
                            for i in range(2):
                                mm = pe.matmul(psum[:, PAIR_BANKS[n % S_SLOTS] + i, :],
                                               k_stack[:, 2 * j + i, t * P:(t + 1) * P],
                                               back(q_stack[:, g, 2 * j + i, :], half * HALF, HALF, N),
                                               start=True, stop=True)
                            mm.then_inc(SEMS["s_mm"], 1)
                    if q >= PV_LAG:
                        t, half = divmod(q - PV_LAG, NHALF)
                        if q == PV_LAG and g == 0:
                            need(pe, "lo_ready", b, 3)
                            need(pe, "fg_lo", b - 1, 2)
                        need(pe, "probs_ready", b, g * SN + (q - PV_LAG + 1) * HP)
                        for h in range(HG):
                            mm = pe.matmul(psum[h * HD:(h + 1) * HD, 4 + half, :],
                                           vT[:, t, (g * HG + h) * HD:(g * HG + h + 1) * HD],
                                           probs[:, ((q - PV_LAG) * HP + h // 2) % P_SLOTS, h % 2, :],
                                           start=(t == 0), stop=(t == NT - 1))
                        mm.then_inc(SEMS["pv_mm"], 1)

            for kind, arg in (("mean", 0), ("var", 0), ("q", 0), ("q", 1), ("k", 0), ("k", 1)):
                do(kind, arg, 0, 1, True, False)

            def element(b, first, last):
                for g in range(G):
                    rows_phase(b, g, first, last)
                    if g == 0:
                        need(pe, "v_ready", b, NT)
                    columns_phase(b, g, first, last)

            batches(pe, element)
            for kind, arg, b in alone(LAYER_1):
                do(kind, arg, b, 1, False, False, tail=True)

        @block.scalar
        def _(act):
            nc.scalar.preload_act_table_set("natural_log_exp_and_others")
            for name in SCALAR:
                act.sem_inc(SEMS[name], per_batch[name])

            def do(kind, arg, b, g, first, tail=False):
                if kind == "square":
                    need(act, "k_stored", b - 1, 16 * G)
                    for k in range(KC):
                        need(act, "centered", b, k + 1)
                        nc.scalar.activation(squares[:, k, :], xn[:, k, :], ACT.Square).then_inc(SEMS["squared"], 1)
                elif kind == "rstd":
                    need(act, "var_mm", b, 1)
                    need(act, "proj_mm", b - 2, KC * NHALF)
                    nc.scalar.activation(lnvar, pair(6), ACT.Ln, bias=eps_col[:, 0:1]).then_inc(SEMS["rstd_ready"], 1)
                    need(act, "rstd_ready", b, 1)
                    nc.scalar.activation(rstd, lnvar, ACT.Exp, scale=-0.5).then_inc(SEMS["rstd_ready"], 1)
                elif kind == "split_q":
                    need(act, "qk_mm", b, 2 * (1 - g) + 1)
                    need(act, "k_stored", b, 16 * (1 - g))
                    nc.scalar.activation(st[:, 0, ::-1], pair(4), ACT.Copy, scale=SCALE).then_inc(SEMS["hi_ready"], 1)
                elif kind == "split_k":
                    need(act, "qk_mm", b, 2 * (1 - g) + 2)
                    need(act, "q_stored", b, 16 * (2 - g))
                    nc.scalar.activation(st[:, 0, :], pair(6), ACT.Copy).then_inc(SEMS["hi_ready"], 1)
                elif kind == "v":
                    if arg == 0:
                        need(act, "pv_mm", b, 0)
                    need(act, "v_mm", b, arg + 1)
                    nc.scalar.copy(vT[:, arg, :], psum[:, 4 + arg % 4, 0:C]).then_inc(SEMS["v_ready"], 1)
                elif kind in ("split_f", "split_g"):
                    t = ("split_f", "split_g").index(kind)
                    need(act, "fg_mm", b, t + 1)
                    need(act, "s1_mm", b, 0)
                    nc.scalar.activation(fg_stack[:, t, :], pair(4)[0:KS], ACT.Identity,
                                         bias=bfg[:, t:t + 1]).then_inc(SEMS["fg_hi"], 1)
                elif kind == "max1":
                    t = arg
                    slot = t % 2 if tail else slot_of(g, first, ("s1", t))
                    need(act, "nmax1_ready", b, t + 1)
                    if t == 0:
                        need(act, "pv_mm", b + 1, 0 if tail else TG)
                    if t >= 2:
                        need(act, "sa_mm", b, t - 1)
                    nc.scalar.activation(attn1[:, t % 2, :], pair(2 * slot), ACT.Exp, bias=nmax1[:, t:t + 1],
                                         accum_out=l1[:, t:t + 1]).then_inc(SEMS["e1_ready"], 1)

            for kind in ("square", "rstd", "split_q", "split_k"):
                do(kind, 0, 0, 1, True)

            def element(b, first, last):
                for g in range(G):
                    for m in range(A_TILES):
                        need(act, "a_max", b, g * A_TILES + m + 1)
                        nc.scalar.activation(biased[:, m % 2, :], biased[:, m % 2, :], ACT.Exp, scale=-1.0,
                                             bias=nmax[:, m:m + 1],
                                             accum_out=rowsum[:, m:m + 1]).then_inc(SEMS["sum_ready"], 1)
                        for kind, arg, e in side_work(g, b, m, first, last):
                            do(kind, arg, e, g, first)
                    need(act, "sum_ready", b, (g + 1) * A_TILES)
                    need(act, "shifted", b, 2 * g)
                    nc.scalar.activation(lnsum[:], rowsum[:], ACT.Ln).then_inc(SEMS["ln_ready"], 1)
                    need(act, "ln_ready", b, 2 * g + 1)
                    nc.scalar.activation(invsum[:], lnsum[:], ACT.Exp, scale=-1.0).then_inc(SEMS["ln_ready"], 1)
                    need(act, "shift_mm", b, g + 1)
                    need(act, "rows_loaded", b, 32 * g)
                    nc.scalar.copy(shift_rows[:], psum[0:2 * HG * NT, 0, 0:P]).then_inc(SEMS["rows_ready"], 1)
                    for n in range(SN):
                        need(act, "bias_added", b, g * SN + n + 1)
                        if n >= P_SLOTS:
                            need(act, "pv_mm", b, g * TG + (n - P_SLOTS) // HP + 1)
                        elif n == 0:
                            need(act, "pv_mm", b, g * TG)
                            need(act, "sa_mm", b - 2 + g, NT)
                        nc.scalar.activation(probs[:, n % P_SLOTS], biased[:, n % 2, :]
                                             .rearrange("p (i n) -> p i n", i=2),
                                             ACT.Exp).then_inc(SEMS["probs_ready"], 1)
                    if g == 0:
                        need(act, "proj_mm", b - 1, KC * NHALF)
                    elif not last:
                        need(act, "normed", b + 1, KC)
                    for half in range(NHALF):
                        need(act, "pv_mm", b, g * TG + TG - NHALF + half + 1)
                        nc.scalar.copy(o[:, g, half * HALF:(half + 1) * HALF],
                                       psum[:, 4 + half, :]).then_inc(SEMS["o_ready"], 1)

            batches(act, element)
            for kind, arg, b in alone(LAYER_1):
                do(kind, arg, b, 1, False, tail=True)

        @block.vector
        def _(dve):
            for name in VECTOR:
                dve.sem_inc(SEMS[name], per_batch[name])
            nc.vector.memset(mean_w[:], 1.0 / C)
            nc.vector.memset(k_stack[KS:KS + 2].bitcast(F32), 1.0)
            nc.vector.memset(eps_col[:], EPS).then_inc(consts_set, 1)
            dve.wait_ge(weights_loaded, 16 * N_WEIGHTS)
            turned = 0

            def turned_in(rows, cols):
                nonlocal turned
                turned += 1
                dve.wait_ge(w_turned, turned)
                return psum[0:cols, (turned - 1) % 8, 0:rows]

            for t in range(3 * KC):
                for k in range(KC):
                    nc.vector.tensor_scalar(wqkvT[:, k, t * P:(t + 1) * P], turned_in(P, P), gamma_col[:, k:k + 1],
                                            None, ALU.mult).then_inc(w_kept, 1)
            for dst in (woutT, whT):
                for t in range(KC):
                    for k in range(KC):
                        nc.vector.tensor_copy(dst[:, k, t * P:(t + 1) * P], turned_in(P, P)).then_inc(w_kept, 1)
            for t in range(2):
                for k in range(KC):
                    src = turned_in(C8, P)
                    for part in range(KS // HD):
                        last = nc.vector.tensor_copy(wfgT[:, k, t, part * HD:(part + 1) * HD], src)
                    last.then_inc(w_kept, 1)
            nc.vector.tensor_copy(w0T, turned_in(D0, 2)).then_inc(w_kept, 1)
            nc.vector.tensor_copy(w1T, turned_in(D0, D0)).then_inc(w_kept, 1)
            nc.vector.tensor_copy(w2T, turned_in(G * HG, D0)).then_inc(w_kept, 1)
            added = 0
            for m in range(MSTEPS):
                for layer, (bank, col, dst) in enumerate(((0, b0_col, h_a), (1, b1_col, h_b))):
                    dve.wait_ge(mlp_mm, 3 * m + layer + 1)
                    nc.vector.tensor_scalar(h_sum, psum[0:D0, bank, 0:MC], col, None,
                                            ALU.add).then_inc(mlp_add, 1)
                    added += 1
                    dve.wait_ge(mlp_add, added)
                    nc.vector.scalar_tensor_tensor(dst, h_sum, LEAK, h_sum, ALU.mult,
                                                   ALU.max).then_inc(mlp_act, 1)
                dve.wait_ge(mlp_mm, 3 * m + 3)
                nc.vector.tensor_scalar(table_sb[:, m * MC:(m + 1) * MC], psum[0:G * HG, 2, 0:MC], b2_col, None, ALU.add).then_inc(table_ready, 1)

            def do(kind, arg, b, g, first, tail=False):
                if kind == "centre":
                    need(dve, "mean_mm", b, 1)
                    for k in range(KC):
                        nc.vector.tensor_tensor(xn[:, k, :], xn[:, k, :], pair(4),
                                                ALU.subtract).then_inc(SEMS["centered"], 1)
                elif kind == "norm":
                    need(dve, "rstd_ready", b, 2)
                    need(dve, "centered", b, KC)
                    for k in range(KC):
                        nc.vector.tensor_tensor(xn[:, k, :], xn[:, k, :], rstd, ALU.mult).then_inc(SEMS["normed"], 1)
                elif kind == "split_q":
                    need(dve, "hi_ready", b, 2 * (1 - g) + 1)
                    nc.vector.scalar_tensor_tensor(st[:, 1, ::-1], pair(4), SCALE, st[:, 0, ::-1].bitcast(F32),
                                                   ALU.mult, ALU.subtract).then_inc(SEMS["lo_ready"], 1)
                elif kind == "split_k":
                    need(dve, "hi_ready", b, 2 * (1 - g) + 2)
                    nc.vector.tensor_tensor(st[:, 1, :], pair(6), st[:, 0, :].bitcast(F32),
                                            ALU.subtract).then_inc(SEMS["lo_ready"], 1)
                elif kind == "add_x":
                    c, half = divmod(arg, NHALF)
                    cols = slice(half * HALF, (half + 1) * HALF)
                    if arg == 0:
                        need(dve, "res_loaded", b, 16)
                    need(dve, "proj_mm", b, arg + 1)
                    nc.vector.tensor_tensor(x1[:, c, cols], x1[:, c, cols], psum[:, 4 + arg % 2, :],
                                            ALU.add).then_inc(SEMS["x1_ready"], 1)
                elif kind in ("split_f", "split_g"):
                    t = ("split_f", "split_g").index(kind)
                    lo = 2 - t
                    rows = slice(lo * HD, (lo + 1) * HD)
                    need(dve, "fg_hi", b, t + 1)
                    nc.vector.scalar_tensor_tensor(fg_stack[rows, t, :], pair(4)[rows], bfg[rows, t:t + 1],
                                                   fg_stack[rows, t, :].bitcast(F32), ALU.add,
                                                   ALU.subtract).then_inc(SEMS["fg_lo"], 1)
                elif kind == "keep_h":
                    if arg == 0:
                        need(dve, "pv_mm", b + 1, 0 if tail else TG)
                    need(dve, "h_mm", b, arg + 1)
                    nc.vector.tensor_tensor(hT[:, arg, :], psum[:, 4 + arg % 2, 0:C], bh_all[:],
                                            ALU.add).then_inc(SEMS["h_ready"], 1)
                elif kind == "max1":
                    slot = arg % 2 if tail else slot_of(g, first, ("s1", arg))
                    need(dve, "s1_mm", b, arg + 1)
                    nc.vector.tensor_reduce(nmax1[:, arg:arg + 1], pair(2 * slot), AX_X, ALU.max,
                                            negate=True).then_inc(SEMS["nmax1_ready"], 1)
                elif kind == "scale_h":
                    need(dve, "e1_ready", b, arg + 1)
                    nc.vector.reciprocal(rl1[:, arg:arg + 1], l1[:, arg:arg + 1]).then_inc(SEMS["rl1_ready"], 1)
                    need(dve, "rl1_ready", b, arg + 1)
                    need(dve, "h_ready", b, NT)
                    if arg >= 2:
                        need(dve, "sa_mm", b, arg - 1)
                    nc.vector.tensor_scalar(hs[:, arg % 2, :], hT[:, arg, :], rl1[:, arg:arg + 1], None,
                                            ALU.mult).then_inc(SEMS["hs_ready"], 1)
                elif kind == "add_y":
                    need(dve, "sa_mm", b, NT)
                    for c in range(KC):
                        for half in range(NHALF):
                            cols = slice(half * HALF, (half + 1) * HALF)
                            nc.vector.scalar_tensor_tensor(x1[:, c, cols], psum[:, 4 + 2 * c + half, :],
                                                           gamma1_col[:, 0:1], x1[:, c, cols], ALU.mult,
                                                           ALU.add).then_inc(SEMS["y_ready"], 1)

            for kind in ("centre", "norm", "split_q", "split_k"):
                do(kind, 0, 0, 1, True)

            def element(b, first, last):
                for g in range(G):
                    for m in range(A_TILES):
                        h, t = divmod(m, NT)
                        a0 = (H - ROWS - ROWS * t) * W
                        free = ("sum_ready", b, g * A_TILES + m - 1) if m >= 2 else ("probs_ready", b, g * SN)
                        need_beside(dve, (lines_loaded, 16 * ROWS), ("a_mm", b, g * A_TILES + m + 1), free)
                        nc.vector.tensor_tensor_reduce(biased[:, m % 2, :], pair(2 * slot_of(g, first, ("a", m))),
                                                       bias_lines[:, g * HG + h, a0:a0 + N], -1.0, BIG, ALU.add,
                                                       ALU.min, nmax[:, m:m + 1]).then_inc(SEMS["a_max"], 1)
                        for kind, arg, e in side_work(g, b, m, first, last):
                            do(kind, arg, e, g, first)
                    need(dve, "a_max", b, (g + 1) * A_TILES)
                    need(dve, "ln_ready", b, 2 * g + 2)
                    need(dve, "shift_mm", b, g)
                    nc.vector.tensor_tensor(shift[:, 0], rowsum[:], invsum[:], ALU.mult).then_inc(SEMS["scaled"], 1)
                    need(dve, "scaled", b, g + 1)
                    nc.vector.scalar_tensor_tensor(shift[:, 1], shift[:, 0], -1.0, lnsum[:], ALU.add,
                                                   ALU.add).then_inc(SEMS["shifted"], 1)
                    need(dve, "shifted", b, 2 * g + 1)
                    nc.vector.tensor_tensor(shift[:, 2], nmax[:], shift[:, 1],
                                            ALU.subtract).then_inc(SEMS["shifted"], 1)
                    need(dve, "shifted", b, 2 * g + 2)
                    nc.vector.tensor_copy(shift_hi[:], shift[:, 2]).then_inc(SEMS["split_hi"], 1)
                    need(dve, "split_hi", b, g + 1)
                    nc.vector.tensor_copy(shift_parts[:, 0], shift_hi[:].bitcast(F32))
                    nc.vector.tensor_tensor(shift_parts[:, 1], shift[:, 2], shift_hi[:].bitcast(F32),
                                            ALU.subtract).then_inc(SEMS["parts_ready"], 1)
                    for kind, arg, e in side_work(g, b, TAIL, first, last):
                        do(kind, arg, e, g, first)
                    for n in range(SN):
                        q, j = divmod(n, HP)
                        t, half = divmod(q, NHALF)
                        a0 = (half * (H // NHALF) - ROWS * t + H - ROWS) * W
                        need(dve, "s_mm", b, g * SN + n + 1)
                        if n >= 2:
                            need(dve, "probs_ready", b, g * SN + n - 1)
                        elif n == 0:
                            need(dve, "sum_ready", b, (g + 1) * A_TILES)
                        bank = PAIR_BANKS[n % S_SLOTS]
                        nc.vector.tensor_tensor(biased[:, n % 2, :].rearrange("p (i n) -> p i n", i=2),
                                                psum[:, bank:bank + 2, :],
                                                bias_lines[:, g * HG + 2 * j:g * HG + 2 * j + 2, a0:a0 + HALF],
                                                ALU.add).then_inc(SEMS["bias_added"], 1)

            batches(dve, element)
            for kind, arg, b in alone(LAYER_1):
                do(kind, arg, b, 1, False, tail=True)


N_WEIGHTS = 16 + 6


def back(ap, start, count, total):
    first = total - 1 - start
    stop = first - count
    return ap[:, first:(stop if stop >= 0 else None):-1]


def tiles_to_turn(square, narrow, small):
    for raw in square:
        for t in range(raw.shape[1]):
            for k in range(raw.shape[2] // P):
                yield raw[:, t, k * P:(k + 1) * P]
    for raw in narrow:
        for k in range(raw.shape[1] // P):
            yield raw[:, k * P:(k + 1) * P]
    yield from small


_INS = ["x", "L0_conv_gamma", "L0_conv_w_qkv", "L0_conv_w_out", "L0_conv_cpb_w0", "L0_conv_cpb_b0",
        "L0_conv_cpb_w1", "L0_conv_cpb_b1", "L0_conv_cpb_w2", "L0_conv_cpb_b2", "L1_conv_Wf", "L1_conv_bf",
        "L1_conv_Wg", "L1_conv_bg", "L1_conv_Wh", "L1_conv_bh", "L1_conv_gamma"]
_OUTS = [((8, 256, 32, 32), "float32")]


def shape_constants(side):
    d = np.arange(1 - side, side, dtype=np.float32)
    line = (np.sign(d) * np.log(np.abs(d) + np.float32(1.0))).astype(np.float32)
    dy, dx = np.meshgrid(line, line, indexing="ij")
    return [np.stack([dy.ravel(), dx.ravel()]), np.eye(P, dtype=np.float32)]


def kernel(**inputs):
    import concourse.bacc as bacc
    from concourse.bass_utils import run_bass_kernel_spmd

    nc = bacc.Bacc("TRN2", target_bir_lowering=False, num_devices=1)
    arrays, args = {}, []
    named = [(n, np.ascontiguousarray(inputs[n])) for n in _INS]
    named += list(zip(("rel_log", "identity"), shape_constants(inputs["x"].shape[2])))
    for name, a in named:
        arrays[f"in_{name}_dram"] = a
        args.append(nc.dram_tensor(f"in_{name}_dram", a.shape, mybir.dt.from_np(a.dtype), kind="ExternalInput").ap())
    for i, (shape, dtype) in enumerate(_OUTS):
        args.append(nc.dram_tensor(f"out_{i}_dram", shape, mybir.dt.from_np(np.dtype(dtype)),
                                   kind="ExternalOutput").ap())
    two_layer_attention(nc, *args)
    r = run_bass_kernel_spmd(nc, [arrays], core_ids=[0])
    return r.results[0]["out_0_dram"]
```

```python
from contextlib import ExitStack

import numpy as np

import concourse.bass as bass
from concourse import mybir

ALU = mybir.AluOpType
ACT = mybir.ActivationFunctionType
AX_X = mybir.AxisListType.X
F32 = mybir.dt.float32
F32R = mybir.dt.float32r

P = 128
HD = 32
HG = P // HD
EPS = 1e-5
LEAK = 0.1
BIG = 3.0e38
BIASED = 3
HP = HG // 2
P_SLOTS = 5
PV_LAG = 2


def two_layer_attention(nc, x, gamma, w_qkv, w_out, w0, b0, w1, b1, w2, b2,
                        Wf, bf, Wg, bg, Wh, bh, gamma1, rel_log, ident_in, out):
    B, C, H, W = x.shape
    N = H * W
    KC = C // P
    NT = N // P
    HALF = 512
    NHALF = N // HALF
    G = C // P
    ROWS = P // W
    DY, DX = 2 * H - 1, 2 * W - 1
    NA = H + (NT - 1) * ROWS
    D0 = w0.shape[0]
    SCALE = HD ** -0.5
    C8 = Wf.shape[0]
    KS = 3 * HD
    TG = NHALF * NT

    x_dram = x.rearrange("b (k p) h w -> b p k (h w)", p=P)
    out_dram = out.rearrange("b (k p) h w -> b p k (h w)", p=P)
    table_dram = nc.dram_tensor("bias_table", [G * HG, DY * DX], F32)
    q_dram = nc.dram_tensor("q_parts", [2, HG, HD, N], F32)
    k_dram = nc.dram_tensor("k_parts", [2, HG, HD, N], F32)
    lines_dram = nc.dram_tensor("bias_lines", [W, G * HG, DY, W], F32)

    with ExitStack() as ctx:
        def sb(name, shape, dt=F32):
            return ctx.enter_context(nc.sbuf_tensor(name, shape, dt))

        def sem(name):
            return ctx.enter_context(nc.semaphore(name))

        psum = ctx.enter_context(nc.psum_tensor("psum", [P, 8, HALF], F32))

        def pair(bank):
            return psum[:, bank:bank + 2, :].rearrange("p a b -> p (a b)")

        ident = sb("ident", [P, P])
        mean_w = sb("mean_w", [P, P])
        eps_col = sb("eps_col", [P, 1])
        wqkvT = sb("wqkvT", [P, KC, 3 * C])
        woutT = sb("woutT", [P, G, C])
        whT = sb("whT", [P, KC, C])
        wfgT = sb("wfgT", [P, KC, 2, KS])
        bfg = sb("bfg", [KS, 2])
        bh_all = sb("bh_all", [P, C])
        gamma_col = sb("gamma_col", [P, KC])
        gamma1_col = sb("gamma1_col", [P, 1])
        bias_lines = sb("bias_lines_sb", [P, G * HG, NA * W])
        xn = sb("xn", [P, KC, N])
        st = sb("st", [P, 2, N], F32R)
        q_stack = sb("q_stack", [KS + 2, G, NHALF, HG, HALF], F32R)
        KMAIN = 3 * N // 4
        k_main = sb("k_main", [KS + 2, HG, KMAIN], F32R)
        k_tail = sb("k_tail", [KS + 2, G, HG, N - KMAIN], F32R)
        vT = sb("vT", [P, NT, C])
        nmax = sb("nmax", [P, HG * NT])
        rowsum = sb("rowsum", [P, HG * NT])
        lnsum = sb("lnsum", [P, HG * NT])
        invsum = sb("invsum", [P, HG * NT])
        shift = sb("shift", [P, HG * NT])
        shift_hi = sb("shift_hi", [P, HG * NT], F32R)
        shift_parts = sb("shift_parts", [P, NHALF, 2, HG * NT // NHALF])
        shift_rows = sb("shift_rows", [HG * NT, NHALF, P], F32R)
        biased = sb("biased", [P, BIASED, N])
        probs = sb("probs", [P, P_SLOTS, 2, HALF])
        o = sb("o", [P, G, N])
        x1 = sb("x1", [P, KC, N])
        fg_stack = sb("fg_stack", [KS, 2, N], F32R)
        nmax1 = sb("nmax1", [P, NT])
        l1 = sb("l1", [P, NT])
        rl1 = sb("rl1", [P, NT])

        squares = st[:].bitcast(F32)
        lnvar = o[:, 1, :]
        rstd = o[:, 1, :]
        attn1 = (probs[:, 0].rearrange("p h n -> p (h n)"), probs[:, 1].rearrange("p h n -> p (h n)"), o[:, 1, :])
        hT = probs[:, 2:4].rearrange("p s h n -> p (s h n)").rearrange("p (t c) -> p t c", c=C)
        HS = 4
        hs = probs[:, 4].rearrange("p h n -> p (h n)").rearrange("p (s c) -> p s c", c=C)

        wraw = probs[:].rearrange("p s h n -> p (s h n)")
        wq_raw = wraw[:, 0:6 * C].rearrange("p (t c) -> p t c", c=C)
        wo_raw = wraw[:, 6 * C:8 * C].rearrange("p (t c) -> p t c", c=C)
        wh_raw = wraw[:, 8 * C:10 * C].rearrange("p (t c) -> p t c", c=C)
        wf_raw = wraw[0:C8, 10 * C:11 * C]
        wg_raw = wraw[0:C8, 11 * C:12 * C]
        mlp = wraw[0:D0, 12 * C:]
        w0T, w1_raw, w1T = mlp[0:2, 0:D0], mlp[:, D0:2 * D0], mlp[:, 2 * D0:3 * D0]
        w2T, w2_raw = mlp[:, 3 * D0:3 * D0 + G * HG], mlp[0:G * HG, 4 * D0:5 * D0]
        b0_col, b1_col = mlp[:, 5 * D0:5 * D0 + 1], mlp[:, 5 * D0 + 1:5 * D0 + 2]
        b2_col = mlp[0:G * HG, 5 * D0 + 2:5 * D0 + 3]
        w0_raw = mlp[:, 6 * D0:6 * D0 + 2]
        room = bias_lines[:].rearrange("p h n -> p (h n)")
        MSTEPS = 9
        MC = DY * DX // MSTEPS
        assert MC * MSTEPS == DY * DX and MC <= HALF
        rel_sb = room[0:2, 0:DY * DX]
        table_sb = room[0:G * HG, DY * DX:2 * DY * DX]
        sum1, sum2, hidden1, hidden2 = (room[0:D0, 2 * DY * DX + 2 * i * MC:2 * DY * DX + 2 * (i + 1) * MC]
                                        .rearrange("p (s n) -> p s n", s=2) for i in range(4))

        weights_loaded = sem("weights_loaded")
        rel_loaded = sem("rel_loaded")
        table_stored = sem("table_stored")
        lines_stored = sem("lines_stored")
        consts_set = sem("consts_set")
        w_turned = sem("w_turned")
        w_kept = sem("w_kept")
        hidden1_mm, hidden1_sum, hidden1_ready = sem("hidden1_mm"), sem("hidden1_sum"), sem("hidden1_ready")
        hidden2_mm, hidden2_sum, hidden2_ready = sem("hidden2_mm"), sem("hidden2_sum"), sem("hidden2_ready")
        table_mm = sem("table_mm")
        table_ready = sem("table_ready")
        credit = {}

        def counted(name, per_batch):
            s = sem(name)
            credit[name] = (s, per_batch)
            return s

        x_loaded = counted("x_loaded", 16)
        res_loaded = counted("res_loaded", 16)
        Q_DMAS = 3 * NHALF * 16
        K_DMAS = 3 * 3 * 16
        q_stored = counted("q_stored", G * 16)
        q_loaded = counted("q_loaded", G * Q_DMAS)
        k_stored = counted("k_stored", G * 16)
        k_loaded = counted("k_loaded", G * K_DMAS)
        rows_loaded = counted("rows_loaded", G * NHALF * 32)
        y_stored = counted("y_stored", 16)
        TENSOR = dict(mean_mm=1, var_mm=1, qk_mm=2 * (NHALF + 1), v_mm=NT, a_mm=G * HG * NT,
                      shift_mm=G * NHALF, s_mm=G * TG * HP,
                      pv_mm=G * TG, proj_mm=KC * NHALF, fg_mm=3, h_mm=NT, s1_mm=NT, sa_mm=NT)
        VECTOR = dict(centered=KC, normed=KC, lo_ready=2 * (NHALF + 1), a_max=G * HG * NT, scaled=G * NHALF,
                      shifted=2 * G * NHALF, split_hi=G * NHALF,
                      parts_ready=G * NHALF, bias_added=G * TG * HP, x1_ready=KC * NHALF, fg_lo=3, h_ready=NT,
                      nmax1_ready=NT, rl1_ready=NT, y_ready=KC * NHALF)
        SCALAR = dict(squared=KC, rstd_ready=2, hi_ready=2 * (NHALF + 1), v_ready=NT,
                      sum_ready=G * HG * NT, ln_ready=2 * G * NHALF,
                      rows_ready=G * NHALF, probs_ready=G * TG * HP, o_ready=G * NHALF, fg_hi=3, e1_ready=NT, hs_ready=NT)
        for kind in (TENSOR, VECTOR, SCALAR):
            for name, n in kind.items():
                counted(name, n)
        lines_loaded = [sem(f"lines_loaded_{h}") for h in range(G * HG)]
        per_batch = {name: k for name, (s, k) in credit.items()}

        SEMS = {name: s for name, (s, k) in credit.items()}
        start = {name: k * (2 if name in ("s_mm", "bias_added", "probs_ready") else 1)
                 for name, k in per_batch.items()}

        def need(eng, name, b, n):
            value = b * per_batch[name] + (start[name] + n)
            if isinstance(value, int):
                if value > 0:
                    eng.wait_ge(SEMS[name], value)
            elif eng is nc.sync:
                need_beside(eng, (lines_stored, 16 * W), (name, b, n))
            else:
                eng.wait_ge(SEMS[name], value)

        def need_beside(eng, constant, *waits):
            values = [(name, b * per_batch[name] + (start[name] + n)) for name, b, n in waits]
            values = [(name, v if isinstance(v, int) else eng.to_reg(v)) for name, v in values]
            eng.wait_ge(*constant)
            for name, v in values:
                eng.wait_ge(SEMS[name], v)

        A_TILES = HG * NT
        HM = A_TILES // NHALF
        QUANTA = 4
        side_0 = [(3 + i, "q", i) for i in range(QUANTA)] + [(6, "high_q", 0), (8, "low_q", 0)]
        side_0 += [(4 + t, "v", t) for t in range(NT)] + [(3 + t, "keep_v", t) for t in range(NT)]
        side_0 += [(11 + i, "k", i) for i in range(QUANTA)] + [(14, "high_k", 0), (16, "low_k", 0)]
        side_0 += [(14 + i, "proj", i) for i in range(KC * NHALF * G)]
        side_0 += [(15 + 2 * j, "add_x", j) for j in range(KC * NHALF)]
        side_0 += [(20 + i, "mean", i) for i in range(QUANTA)] + [(23, "centre", 0), (24, "square", 0)]
        side_0 += [(24 + i, "f", i) for i in range(QUANTA)] + [(27, "high_f", 0), (29, "low_f", 0)]
        side_0 += [(27 + i, "var", i) for i in range(QUANTA)] + [(30, "rstd", 0)]
        side_1 = [(3 + t, "h", t) for t in range(NT)] + [(3 + t, "keep_h", t) for t in range(NT)]
        for t in range(NT):
            at = 6 + 8 * t // 3
            side_1 += [(at, "s1", t), (at, "max1", t), (at, "exp1", t), (at + 2, "invert", t), (at + 2, "scale_h", t)]
            side_1 += [(at + 4 + i, "sa", QUANTA * t + i) for i in range(QUANTA)]
        for side, at in ((side_0, HM), (side_1, HM + 2)):
            side += [(at, "ln", 0), (at + 2, "shift", 0), (at + 5, "turn", 0), (at + 4, "keep_rows", 0)]
        column_0 = [(1, "rstd", 1), (3, "norm", 0), (9, "norm", 1)]
        column_0 += [(4, "shift", 1), (6, "turn", 1), (6, "keep_rows", 1)]
        for kind, half, one, two in (("g", 0, 2, 4), ("g", 1, 8, 10), ("k0", 0, 14, 16), ("k0", 1, 24, 26)):
            column_0 += [(one, kind, 2 * half), (two, kind, 2 * half + 1), (two + 1, "high_" + kind, half),
                         (two + 3, "low_" + kind, half)]
        column_1 = [(i // 2, "add_y", i) for i in range(KC * NHALF)]
        column_1 += [(4, "shift", 1), (7, "turn", 1), (6, "keep_rows", 1)]
        for kind, half, one, two in (("q0", 0, 4, 6), ("q0", 1, 12, 14)):
            column_1 += [(one, kind, 2 * half), (two, kind, 2 * half + 1), (two + 1, "high_" + kind, half),
                         (two + 3, "low_" + kind, half)]
        SIDES = {(0, "rows"): side_0, (0, "columns"): column_0, (1, "rows"): side_1, (1, "columns"): column_1}
        LAYER_1 = ("proj", "add_x", "f", "high_f", "low_f", "g", "high_g", "low_g", "h", "keep_h", "s1", "max1",
                   "exp1", "invert", "scale_h", "sa", "add_y")
        AHEAD = ("mean", "centre", "square", "var", "rstd", "norm", "q0", "high_q0", "low_q0", "k0", "high_k0",
                 "low_k0")

        def side_work(g, phase, n, b, first, last):
            for at, kind, arg in SIDES[g, phase]:
                if at != n:
                    continue
                if kind in LAYER_1:
                    if not first:
                        yield kind, arg, b - 1
                elif kind in AHEAD:
                    if not last:
                        yield kind, arg, b + 1
                else:
                    yield kind, arg, b

        SN = TG * HP
        S_SLOTS = 3

        def ring(g, first):
            items = []
            for phase, count in (("rows", A_TILES), ("columns", SN)):
                for n in range(count):
                    items.append((phase, n))
                    for at, kind, arg in SIDES[g, phase]:
                        if at == n and (kind == "turn" or (kind == "s1" and not first)):
                            items.append((kind, arg))
            columns = items.index(("columns", 0))
            assert (len(items) - columns) % S_SLOTS == 0
            banks = [(0, 2)[(n - columns) % 2] for n in range(columns)]
            banks += [(0, 2, 6)[(n - columns) % S_SLOTS] for n in range(columns, len(items))]
            return items, banks

        def bank_of(g, first, item):
            items, banks = ring(g, first)
            return banks[items.index(item)]

        def before_in_bank(g, first, item):
            items, banks = ring(g, first)
            n = items.index(item)
            before = [i for i in range(n) if banks[i] == banks[n]]
            return items[before[-1]] if before else None

        def alone(kinds):
            for schedule in SIDES.values():
                for at, kind, arg in sorted(schedule, key=lambda entry: entry[0]):
                    if kind in kinds:
                        yield kind, arg, B - 1

        def batches(eng, body):
            body(0, first=True, last=False)
            with eng.Fori(1, B - 1) as b:
                body(b, first=False, last=False)
            body(B - 1, first=False, last=True)

        def row_tile(m):
            r, rest = divmod(m, HM)
            h, t = divmod(rest, NT // NHALF)
            return r, h, (NHALF - 1 - r) * (NT // NHALF) + t

        def column_tile(n):
            q, j = divmod(n, HP)
            half, t = divmod(q, NT)
            return half, t, j

        KCHUNKS = (0, N // 2, KMAIN, N)
        LEAD = 3

        def last_in_slot(n):
            return SN - (SN - 1 - n) % BIASED

        def split(g, t, half=NHALF - 1):
            return (1 - t) * NHALF + half + 1 if g == 0 else 2 * NHALF + t + 1

        block = ctx.enter_context(nc.Block())

        @block.sync
        def _(sp):
            for name in ("x_loaded", "res_loaded", "q_stored", "q_loaded", "k_stored", "k_loaded", "rows_loaded",
                         "y_stored"):
                sp.sem_inc(SEMS[name], start[name])
            sp.dma_start(xn[:], x_dram[0]).then_inc(x_loaded, 16)
            n = 0
            for dst, src in (
                (ident[:], ident_in),
                (wq_raw, w_qkv.rearrange("(t p) c -> p t c", p=P)),
                (wo_raw, w_out.rearrange("(t p) c -> p t c", p=P)),
                (wh_raw, Wh.rearrange("(t p) c -> p t c", p=P)),
                (wf_raw, Wf), (wg_raw, Wg),
                (bh_all[:], bh.rearrange("(a c) -> a c", a=1).broadcast_to((P, C))),
                (gamma_col[:, 0:1], gamma[0, 0:P].rearrange("p a b -> p (a b)")),
                (gamma_col[:, 1:2], gamma[0, P:2 * P].rearrange("p a b -> p (a b)")),
                (gamma1_col[:], gamma1.rearrange("(a b) -> a b", a=1).broadcast_to((P, 1))),
                (w0_raw, w0), (w1_raw, w1), (w2_raw, w2),
                (b0_col, b0.rearrange("(a b) -> a b", b=1)),
                (b1_col, b1.rearrange("(a b) -> a b", b=1)),
                (b2_col, b2.rearrange("(a b) -> a b", b=1)),
            ):
                sp.dma_start(dst, src).then_inc(weights_loaded, 16)
                n += 1
            for part in range(KS // HD):
                sp.dma_start(bfg[part * HD:(part + 1) * HD, 0:1],
                             bf.rearrange("(a b) -> a b", b=1)).then_inc(weights_loaded, 16)
                sp.dma_start(bfg[part * HD:(part + 1) * HD, 1:2],
                             bg.rearrange("(a b) -> a b", b=1)).then_inc(weights_loaded, 16)
                n += 2
            assert n == N_WEIGHTS
            sp.dma_start(rel_sb, rel_log).then_inc(rel_loaded, 16)

            def through_dram(dram, store_sem):
                sp.dma_start(dram.ap().rearrange("l h d n -> (h d) l n"), st[:].bitcast(F32)).then_inc(store_sem, 16)

            def q_out(b, g):
                need(sp, "lo_ready", b, split(g, 0))
                need(sp, "q_loaded", b, g * Q_DMAS)
                through_dram(q_dram, q_stored)

            def q_in(b, g, done):
                need(sp, "q_stored", b, 16 * (g + 1))
                need(sp, *done)
                for r, part in enumerate((0, 0, 1)):
                    for half in range(NHALF):
                        sp.dma_start(q_stack[r * HD:(r + 1) * HD, g, half].bitcast(F32),
                                     q_dram.ap()[part, :, :, half * HALF:(half + 1) * HALF]
                                     .rearrange("h d n -> d h n")).then_inc(q_loaded, 16)

            def k_out(b, g):
                need(sp, "lo_ready", b, split(g, 1))
                need(sp, "k_loaded", b, g * K_DMAS)
                through_dram(k_dram, k_stored)

            def k_in(b, g, chunk):
                need(sp, "k_stored", b, 16 * (g + 1))
                cols = slice(KCHUNKS[chunk], KCHUNKS[chunk + 1])
                dst = k_main[:, :, cols] if cols.start < KMAIN else k_tail[:, g]
                for r, part in enumerate((0, 1, 0)):
                    sp.dma_start(dst[r * HD:(r + 1) * HD].bitcast(F32),
                                 k_dram.ap()[part, :, :, cols].rearrange("h d n -> d h n")).then_inc(k_loaded, 16)

            def shift_to_stack(b, g, r):
                need(sp, "rows_ready", b, g * NHALF + r + 1)
                for part in range(2):
                    sp.dma_start(q_stack[KS + part:KS + part + 1, g, NHALF - 1 - r].bitcast(F32)
                                 .rearrange("p h (t n) -> p (h t) n", n=P),
                                 shift_rows[part * HM:(part + 1) * HM, r, :].bitcast(F32)).then_inc(rows_loaded, 16)

            def residual_in(b):
                need(sp, "y_stored", b, 0)
                sp.dma_start(x1[:], x_dram[b]).then_inc(res_loaded, 16)

            def result_out(b):
                need(sp, "y_ready", b, KC * NHALF)
                sp.dma_start(out_dram[b], x1[:]).then_inc(y_stored, 16)

            sp.wait_ge(table_ready, MSTEPS)
            sp.dma_start(table_dram.ap(), table_sb).then_inc(table_stored, 16)
            sp.wait_ge(table_stored, 16)
            for x in range(W):
                src = table_dram.ap().rearrange("h (a w) -> h a w", w=DX)[:, :, W - 1 - x:2 * W - 1 - x]
                sp.dma_start(lines_dram.ap()[x], src).then_inc(lines_stored, 16)
                if x == W // 2:
                    k_out(0, 0)
            q_out(0, 0)
            for chunk in (2, 0, 1):
                k_in(0, 0, chunk)
            q_in(0, 0, ("s_mm", -1, SN))
            sp.wait_ge(lines_stored, 16 * W)
            for h in range(G * HG):
                for yl in range(ROWS):
                    sp.dma_start(bias_lines[yl * W:(yl + 1) * W, h],
                                 lines_dram.ap()[:, h, ROWS - 1 - yl:ROWS - 1 - yl + NA]
                                 .rearrange("x a w -> x (a w)")).then_inc(lines_loaded[h], 16)

            def columns_done(b, g, chunk):
                need(sp, "s_mm", b, g * SN + (SN - SN // NHALF) + KCHUNKS[chunk + 1] // P * HP)

            def element(b, first, last):
                q_out(b, 1)
                q_in(b, 1, ("s_mm", b, 0))
                if not last:
                    need(sp, "v_mm", b, NT)
                    need(sp, "qk_mm", b, split(1, 1))
                    sp.dma_start(xn[:], x_dram[b + 1]).then_inc(x_loaded, 16)
                k_out(b, 1)
                k_in(b, 1, 2)
                for r in range(NHALF):
                    shift_to_stack(b, 0, r)
                for chunk in range(2):
                    columns_done(b, 0, chunk)
                    k_in(b, 1, chunk)
                if not last:
                    k_out(b + 1, 0)
                    need(sp, "s_mm", b, SN)
                    k_in(b + 1, 0, 2)
                for r in range(NHALF):
                    shift_to_stack(b, 1, r)
                if not first:
                    result_out(b - 1)
                if not last:
                    q_out(b + 1, 0)
                    q_in(b + 1, 0, ("s_mm", b, SN))
                if not last:
                    for chunk in range(2):
                        columns_done(b, 1, chunk)
                        k_in(b + 1, 0, chunk)
                residual_in(b)

            batches(sp, element)
            result_out(B - 1)
            sp.wait_ge(y_stored, 16 * (B + 1))

        @block.tensor
        def _(pe):
            for name in TENSOR:
                pe.sem_inc(SEMS[name], start[name])
            pe.wait_ge(weights_loaded, 16 * N_WEIGHTS)
            pe.wait_ge(consts_set, 1)
            turned = 0
            for src in tiles_to_turn((wq_raw, wo_raw, wh_raw), (wf_raw, wg_raw), (w0_raw, w1_raw, w2_raw)):
                rows, cols = src.shape
                if turned >= 8:
                    pe.wait_ge(w_kept, turned - 7)
                pe.transpose(psum[0:cols, turned % 8, 0:rows], src, ident[0:rows, 0:rows]).then_inc(w_turned, 1)
                turned += 1
            pe.wait_ge(w_kept, turned)
            def product(quantum, bank, lhsT, src, done, rows=P):
                half, k = divmod(quantum, KC)
                mm = pe.matmul(psum[0:rows, bank + half, :], lhsT(k), src[:, k, half * HALF:(half + 1) * HALF],
                               start=(k == 0), stop=(k == KC - 1))
                if quantum == NHALF * KC - 1:
                    mm.then_inc(SEMS[done], 1)

            def do(kind, arg, b, g, first, last, tail=False):
                if kind == "mean":
                    if arg == 0:
                        need(pe, "x_loaded", b, 16)
                        need(pe, "lo_ready", b - 1, split(1, 1))
                    product(arg, 6, lambda k: mean_w[:], xn, "mean_mm")
                elif kind == "var":
                    if arg == 0:
                        need(pe, "squared", b, KC)
                    product(arg, 6, lambda k: mean_w[:], squares, "var_mm")
                elif kind in ("q", "k"):
                    t = ("q", "k").index(kind)
                    if arg == 0:
                        need(pe, "normed", b, KC)
                        if t == 0:
                            need(pe, "bias_added", b, 0)
                        else:
                            need(pe, "lo_ready", b, split(1, 0))
                    product(arg, 6, lambda k: wqkvT[:, k, t * C + P:t * C + 2 * P], xn, "qk_mm")
                elif kind in ("q0", "k0"):
                    t = ("q0", "k0").index(kind)
                    half, k = divmod(arg, KC)
                    bank = 5 - t * half
                    if k == 0:
                        need(pe, "normed", b, KC)
                        if t == 0 and half:
                            need(pe, "lo_ready", b, split(0, 0, 0))
                        elif t == 0:
                            need(pe, "lo_ready", b, split(0, 1, 0))
                            need(pe, "y_ready", b - 2, KC * NHALF)
                            need(pe, "o_ready", b - 1, NHALF)
                        elif half:
                            need(pe, "o_ready", b - 1, 1)
                        else:
                            need(pe, "fg_lo", b - 2, 3)
                            need(pe, "v_ready", b - 1, NT)
                    mm = pe.matmul(psum[:, bank, :], wqkvT[:, k, t * C:t * C + P],
                                   xn[:, k, half * HALF:(half + 1) * HALF], start=(k == 0), stop=(k == KC - 1))
                    if k == KC - 1:
                        mm.then_inc(SEMS["qk_mm"], 1)
                elif kind == "v":
                    if arg == 0:
                        need(pe, "o_ready", b, 0)
                    elif arg >= 2:
                        need(pe, "v_ready", b, arg - 1)
                    for k in range(KC):
                        mm = pe.matmul(psum[:, 4 + arg % 2, 0:C], xn[:, k, arg * P:(arg + 1) * P],
                                       wqkvT[:, k, 2 * C:3 * C], start=(k == 0), stop=(k == KC - 1))
                    mm.then_inc(SEMS["v_mm"], 1)
                elif kind == "proj":
                    j, gg = divmod(arg, G)
                    c, half = divmod(j, NHALF)
                    if arg == 0:
                        need(pe, "o_ready", b, G * NHALF)
                        if not tail:
                            need(pe, "v_ready", b + 1, NT)
                    elif j >= 2 and gg == 0:
                        need(pe, "x1_ready", b, j - 1)
                    mm = pe.matmul(psum[:, 4 + j % 2, :], woutT[:, gg, c * P:(c + 1) * P],
                                   o[:, gg, half * HALF:(half + 1) * HALF], start=(gg == 0), stop=(gg == G - 1))
                    if gg == G - 1:
                        mm.then_inc(SEMS["proj_mm"], 1)
                elif kind == "f":
                    if arg == 0:
                        need(pe, "x1_ready", b, KC * NHALF)
                    product(arg, 4, lambda k: wfgT[:, k, 0, :], x1, "fg_mm", rows=KS)
                elif kind == "g":
                    half, k = divmod(arg, KC)
                    if k == 0:
                        need(pe, "fg_lo", b, half + 1)
                    mm = pe.matmul(psum[0:KS, 5, :], wfgT[:, k, 1, :], x1[:, k, half * HALF:(half + 1) * HALF],
                                   start=(k == 0), stop=(k == KC - 1))
                    if k == KC - 1:
                        mm.then_inc(SEMS["fg_mm"], 1)
                elif kind == "h":
                    if arg >= 2:
                        need(pe, "h_ready", b, arg - 1)
                    elif tail:
                        need(pe, "bias_added", b, G * SN)
                    else:
                        need(pe, "bias_added", b + 1, SN)
                    for k in range(KC):
                        mm = pe.matmul(psum[:, 6 + arg % 2, 0:C], x1[:, k, arg * P:(arg + 1) * P], whT[:, k, :],
                                       start=(k == 0), stop=(k == KC - 1))
                    mm.then_inc(SEMS["h_mm"], 1)
                elif kind == "s1":
                    if arg == 0:
                        need(pe, "fg_lo", b, 3)
                    if tail:
                        bank = 2 * (arg % 2)
                        if arg < 2:
                            need(pe, "bias_added", b, G * SN)
                        else:
                            need(pe, "nmax1_ready", b, arg - 1)
                    else:
                        bank = free_bank(("s1", arg), b + 1, g, first, last)
                    for half in range(NHALF):
                        mm = pe.matmul(psum[:, bank + half, :], fg_stack[:, 0, arg * P:(arg + 1) * P],
                                       fg_stack[:, 1, half * HALF:(half + 1) * HALF], start=True, stop=True)
                    mm.then_inc(SEMS["s1_mm"], 1)
                elif kind == "sa":
                    t, i = divmod(arg, QUANTA)
                    c, half = divmod(i, NHALF)
                    if arg == 0 and tail:
                        need(pe, "fg_lo", b, 3)
                    elif arg == 0:
                        need(pe, "o_ready", b + 1, NHALF)
                        if not last:
                            need(pe, "lo_ready", b + 2, split(0, 1))
                    elif arg == NHALF:
                        need(pe, "h_ready", b, NT)
                    if i == 0:
                        need(pe, "hs_ready", b, t + 1)
                    mm = pe.matmul(psum[:, 4 + 2 * c + half, :], hs[:, t % HS, c * P:(c + 1) * P],
                                   attn1[t % 3][:, half * HALF:(half + 1) * HALF],
                                   start=(t == 0), stop=(t == NT - 1))
                    if i == QUANTA - 1:
                        mm.then_inc(SEMS["sa_mm"], 1)

            def free_bank(item, b, g, first, last):
                before = before_in_bank(g, first, item)
                if before is not None:
                    kind, n = before
                    if kind == "rows":
                        need(pe, "a_max", b, g * A_TILES + n + 1)
                    elif kind == "s1":
                        need(pe, "nmax1_ready", b - 1, n + 1)
                    elif kind == "turn":
                        need(pe, "rows_ready", b, g * NHALF + n + 1)
                    else:
                        need(pe, "bias_added", b, g * SN + n + 1)
                elif item[0] == "rows":
                    need(pe, "bias_added", b, g * SN - (2 if bank_of(g, first, item) == 0 else 1))
                elif g == 0:
                    if last:
                        need(pe, "lo_ready", b, split(1, 1))
                    else:
                        need(pe, "rstd_ready", b + 1, 1)
                elif first:
                    need(pe, "bias_added", b, SN)
                else:
                    need(pe, "y_ready", b - 1, NHALF)
                return bank_of(g, first, item)

            def beside(g, phase, n, b, first, last):
                for kind, arg, e in side_work(g, phase, n, b, first, last):
                    if kind == "turn":
                        bank = free_bank((kind, arg), b, g, first, last)
                        need(pe, "parts_ready", b, g * NHALF + arg + 1)
                        pe.matmul(psum[0:2 * HM, bank, 0:P], shift_parts[:, arg].rearrange("p l m -> p (l m)"),
                                  ident[:], start=True, stop=True).then_inc(SEMS["shift_mm"], 1)
                    else:
                        do(kind, arg, e, g, first, last)

            def row_tiles(b, g, first, m):
                if m == 0:
                    need(pe, "q_loaded", b, (g + 1) * Q_DMAS)
                    need(pe, "k_loaded", b, (g + 1) * K_DMAS)
                r, h, t = row_tile(m)
                bank = free_bank(("rows", m), b, g, first, False)
                lhsT = q_stack[0:KS, g, t * P // HALF, h, t * P % HALF:t * P % HALF + P]
                main, tail = k_main[0:KS, h, :], k_tail[0:KS, g, h, :]
                keys = N - KMAIN
                pe.matmul(psum[:, bank, 0:keys], lhsT, tail[:, ::-1], start=True, stop=True)
                pe.matmul(psum[:, bank, keys:HALF], lhsT, back(main, 0, HALF - keys, KMAIN), start=True, stop=True)
                pe.matmul(psum[:, bank + 1, :], lhsT, back(main, HALF - keys, HALF, KMAIN), start=True,
                          stop=True).then_inc(SEMS["a_mm"], 1)

            def rows_phase(b, g, first, last):
                for m in range(A_TILES):
                    if m >= LEAD:
                        row_tiles(b, g, first, m)
                    beside(g, "rows", m, b, first, last)

            def key_tile(g, h, t):
                if t * P < KMAIN:
                    return k_main[:, h, t * P:(t + 1) * P]
                return k_tail[:, g, h, t * P - KMAIN:(t + 1) * P - KMAIN]

            def columns_phase(b, g, first, last):
                for q in range(TG + PV_LAG):
                    if q < TG:
                        for n in range(q * HP, (q + 1) * HP):
                            half, t, j = column_tile(n)
                            if q % NT == 0:
                                need(pe, "rows_loaded", b, (g * NHALF + half + 1) * 32)
                            bank = free_bank(("columns", n), b, g, first, last)
                            for i in range(2):
                                mm = pe.matmul(psum[:, bank + i, :], key_tile(g, 2 * j + i, t),
                                               q_stack[:, g, NHALF - 1 - half, 2 * j + i, ::-1],
                                               start=True, stop=True)
                            mm.then_inc(SEMS["s_mm"], 1)
                            beside(g, "columns", n, b, first, last)
                    for m in (range(LEAD - 1) if q == TG else (LEAD - 1,) if q == TG + 1 else ()):
                        if g == 0:
                            row_tiles(b, 1, first, m)
                        elif not last:
                            row_tiles(b + 1, 0, False, m)
                    if q >= PV_LAG:
                        half, t = divmod(q - PV_LAG, NT)
                        if t == 0:
                            if g == 0:
                                need(pe, "v_ready", b, NT)
                                if not first:
                                    need(pe, "fg_lo", b - 1, 1 + 2 * half)
                                if half and not last:
                                    need(pe, "lo_ready", b + 1, split(0, 1, 0))
                            else:
                                need(pe, "y_ready", b - 1, NHALF + half + 1)
                                need(pe, "o_ready", b, half + 1)
                                if not last:
                                    need(pe, "lo_ready", b + 1, split(0, 1 - half))
                        need(pe, "probs_ready", b, g * SN + (q - PV_LAG + 1) * HP)
                        for h in range(HG):
                            mm = pe.matmul(psum[h * HD:(h + 1) * HD, 4 + half, :],
                                           vT[:, t, (g * HG + h) * HD:(g * HG + h + 1) * HD],
                                           probs[:, ((q - PV_LAG) * HP + h // 2) % P_SLOTS, h % 2, :],
                                           start=(t == 0), stop=(t == NT - 1))
                        mm.then_inc(SEMS["pv_mm"], 1)

            pe.wait_ge(rel_loaded, 16)
            for step in range(MSTEPS + 2):
                m = step
                if m < MSTEPS:
                    if m >= 2:
                        pe.wait_ge(hidden1_sum, m - 1)
                    pe.matmul(psum[0:D0, m % 2, 0:MC], w0T, rel_sb[:, m * MC:(m + 1) * MC], start=True,
                              stop=True).then_inc(hidden1_mm, 1)
                m = step - 1
                if 0 <= m < MSTEPS:
                    pe.wait_ge(hidden1_ready, m + 1)
                    if m >= 2:
                        pe.wait_ge(hidden2_sum, m - 1)
                    pe.matmul(psum[0:D0, 2 + m % 2, 0:MC], w1T, hidden1[:, m % 2], start=True,
                              stop=True).then_inc(hidden2_mm, 1)
                m = step - 2
                if m >= 0:
                    pe.wait_ge(hidden2_ready, m + 1)
                    if m >= 2:
                        pe.wait_ge(table_ready, m - 1)
                    pe.matmul(psum[0:G * HG, 4 + m % 2, 0:MC], w2T, hidden2[:, m % 2], start=True,
                              stop=True).then_inc(table_mm, 1)
                for at, kind in ((1, "mean"), (4, "var")):
                    if step == at:
                        for quantum in range(QUANTA):
                            do(kind, quantum, 0, 1, True, False)
            pe.wait_ge(table_ready, MSTEPS)
            for kind in ("k0", "q0"):
                for quantum in range(QUANTA):
                    do(kind, quantum, 0, 1, True, False)

            for m in range(LEAD):
                row_tiles(0, 0, True, m)

            def element(b, first, last):
                for g in range(G):
                    rows_phase(b, g, first, last)
                    columns_phase(b, g, first, last)

            batches(pe, element)
            for kind, arg, b in alone(LAYER_1):
                do(kind, arg, b, 1, False, False, tail=True)

        @block.scalar
        def _(act):
            nc.scalar.preload_act_table_set("natural_log_exp_and_others")
            for name in SCALAR:
                act.sem_inc(SEMS[name], start[name])

            def do(kind, arg, b, g, first, last, tail=False):
                if kind == "square":
                    need(act, "k_stored", b - 1, 16 * G)
                    for k in range(KC):
                        need(act, "centered", b, k + 1)
                        nc.scalar.activation(squares[:, k, :], xn[:, k, :], ACT.Square).then_inc(SEMS["squared"], 1)
                elif kind == "rstd":
                    if arg == 1:
                        need(act, "rstd_ready", b, 1)
                        nc.scalar.activation(rstd, lnvar, ACT.Exp, scale=-0.5).then_inc(SEMS["rstd_ready"], 1)
                        return
                    need(act, "var_mm", b, 1)
                    need(act, "proj_mm", b - 2, KC * NHALF)
                    nc.scalar.activation(lnvar, pair(6), ACT.Ln, bias=eps_col[:, 0:1]).then_inc(SEMS["rstd_ready"], 1)
                elif kind == "high_q":
                    need(act, "qk_mm", b, split(1, 0))
                    need(act, "q_stored", b, 16)
                    nc.scalar.activation(st[:, 0, ::-1], pair(6), ACT.Copy, scale=SCALE).then_inc(SEMS["hi_ready"], 1)
                elif kind == "high_k":
                    need(act, "qk_mm", b, split(1, 1))
                    need(act, "q_stored", b, 16 * G)
                    nc.scalar.activation(st[:, 0, :], pair(6), ACT.Copy).then_inc(SEMS["hi_ready"], 1)
                elif kind == "high_q0":
                    need(act, "qk_mm", b, split(0, 0, arg))
                    need(act, "k_stored", b, 16)
                    nc.scalar.activation(back(st[:, 0, :], arg * HALF, HALF, N), psum[:, 5, :], ACT.Copy,
                                         scale=SCALE).then_inc(SEMS["hi_ready"], 1)
                elif kind == "high_k0":
                    need(act, "qk_mm", b, split(0, 1, arg))
                    nc.scalar.activation(st[:, 0, arg * HALF:(arg + 1) * HALF], psum[:, 5 - arg, :],
                                         ACT.Copy).then_inc(SEMS["hi_ready"], 1)
                elif kind == "keep_v":
                    if arg == 0:
                        need(act, "pv_mm", b, 0)
                    need(act, "v_mm", b, arg + 1)
                    nc.scalar.copy(vT[:, arg, :], psum[:, 4 + arg % 2, 0:C]).then_inc(SEMS["v_ready"], 1)
                elif kind == "high_f":
                    need(act, "fg_mm", b, 1)
                    need(act, "s1_mm", b, 0)
                    nc.scalar.activation(fg_stack[:, 0, :], pair(4)[0:KS], ACT.Identity,
                                         bias=bfg[:, 0:1]).then_inc(SEMS["fg_hi"], 1)
                elif kind == "high_g":
                    need(act, "fg_mm", b, arg + 2)
                    nc.scalar.activation(fg_stack[:, 1, arg * HALF:(arg + 1) * HALF], psum[0:KS, 5, :], ACT.Identity,
                                         bias=bfg[:, 1:2]).then_inc(SEMS["fg_hi"], 1)
                elif kind == "ln":
                    u = g * NHALF + arg
                    cols = slice(arg * HM, (arg + 1) * HM)
                    need(act, "sum_ready", b, g * A_TILES + (arg + 1) * HM)
                    need(act, "shifted", b, 2 * u - 2)
                    nc.scalar.activation(lnsum[:, cols], rowsum[:, cols], ACT.Ln).then_inc(SEMS["ln_ready"], 1)
                    need(act, "ln_ready", b, 2 * u + 1)
                    nc.scalar.activation(invsum[:, cols], lnsum[:, cols], ACT.Exp,
                                         scale=-1.0).then_inc(SEMS["ln_ready"], 1)
                elif kind == "keep_rows":
                    u = g * NHALF + arg
                    need(act, "shift_mm", b, u + 1)
                    need(act, "rows_loaded", b, 32 * (u - 1))
                    nc.scalar.copy(shift_rows[:, arg, :],
                                   psum[0:2 * HM, bank_of(g, first, ("turn", arg)),
                                        0:P]).then_inc(SEMS["rows_ready"], 1)
                elif kind == "exp1":
                    need(act, "nmax1_ready", b, arg + 1)
                    nc.scalar.activation(attn1[arg % 3], attn1[arg % 3], ACT.Exp, scale=-1.0,
                                         bias=nmax1[:, arg:arg + 1],
                                         accum_out=l1[:, arg:arg + 1]).then_inc(SEMS["e1_ready"], 1)

                elif kind == "scale_h":
                    need(act, "rl1_ready", b, arg + 1)
                    need(act, "h_ready", b, arg + 1)
                    if arg >= HS:
                        need(act, "sa_mm", b, arg - HS + 1)
                    nc.scalar.activation(hs[:, arg % HS, :], hT[:, arg, :], ACT.Copy,
                                         scale=rl1[:, arg:arg + 1]).then_inc(SEMS["hs_ready"], 1)

            def output(b, g, half, last):
                if g == 0:
                    need(act, "proj_mm", b - 1, KC * NHALF)
                else:
                    need(act, "sa_mm", b - 1, NT)
                    if not last:
                        need(act, "normed", b + 1, KC)
                need(act, "pv_mm", b, g * TG + (half + 1) * NT)
                nc.scalar.copy(o[:, g, half * HALF:(half + 1) * HALF],
                               psum[:, 4 + half, :]).then_inc(SEMS["o_ready"], 1)

            act.wait_ge(weights_loaded, 16 * N_WEIGHTS)
            for step in range(MSTEPS + 1):
                m = step
                if m < MSTEPS:
                    act.wait_ge(hidden1_mm, m + 1)
                    if m >= 2:
                        act.wait_ge(hidden1_ready, m - 1)
                    nc.scalar.activation(sum1[:, m % 2], psum[0:D0, m % 2, 0:MC], ACT.Identity,
                                         bias=b0_col).then_inc(hidden1_sum, 1)
                m = step - 1
                if m >= 0:
                    act.wait_ge(hidden2_mm, m + 1)
                    if m >= 2:
                        act.wait_ge(hidden2_ready, m - 1)
                    nc.scalar.activation(sum2[:, m % 2], psum[0:D0, 2 + m % 2, 0:MC], ACT.Identity,
                                         bias=b1_col).then_inc(hidden2_sum, 1)
                for at, kind, arg in ((2, "square", 0), (5, "rstd", 0), (5, "rstd", 1)):
                    if step == at:
                        do(kind, arg, 0, 1, True, False)
            for kind, arg in (("high_k0", 0), ("high_k0", 1), ("high_q0", 0), ("high_q0", 1)):
                do(kind, arg, 0, 1, True, False)

            def element(b, first, last):
                for g in range(G):
                    for m in range(A_TILES):
                        need(act, "a_max", b, g * A_TILES + m + 1)
                        nc.scalar.activation(biased[:, m % BIASED, :], biased[:, m % BIASED, :], ACT.Exp, scale=-1.0,
                                             bias=nmax[:, m:m + 1],
                                             accum_out=rowsum[:, m:m + 1]).then_inc(SEMS["sum_ready"], 1)
                        if m == 2 and g == 1:
                            output(b, 0, 1, last)
                        elif m == 2 and not first:
                            output(b - 1, 1, 1, False)
                        for kind, arg, e in side_work(g, "rows", m, b, first, last):
                            do(kind, arg, e, g, first, last)
                    do("ln", 1, b, g, first, last)
                    for n in range(SN):
                        need(act, "bias_added", b, g * SN + n + 1)
                        if n >= P_SLOTS:
                            need(act, "pv_mm", b, g * TG + (n - P_SLOTS) // HP + 1)
                        elif n == 0:
                            need(act, "pv_mm", b, g * TG)
                            need(act, "sa_mm", b - 2 + g, NT)
                        nc.scalar.activation(probs[:, n % P_SLOTS], biased[:, n % BIASED, :]
                                             .rearrange("p (i n) -> p i n", i=2),
                                             ACT.Exp).then_inc(SEMS["probs_ready"], 1)
                        if n == SN // NHALF + (PV_LAG + 1) * HP - 1:
                            output(b, g, 0, last)
                        for kind, arg, e in side_work(g, "columns", n, b, first, last):
                            do(kind, arg, e, g, first, last)
                if last:
                    output(b, 1, 1, last)

            batches(act, element)
            for kind, arg, b in alone(LAYER_1):
                do(kind, arg, b, 1, False, False, tail=True)

        @block.vector
        def _(dve):
            for name in VECTOR:
                dve.sem_inc(SEMS[name], start[name])
            nc.vector.memset(mean_w[:], 1.0 / C)
            nc.vector.memset(k_main[KS:KS + 2].bitcast(F32), 1.0)
            nc.vector.memset(k_tail[KS:KS + 2].bitcast(F32), 1.0)
            nc.vector.memset(eps_col[:], EPS).then_inc(consts_set, 1)
            dve.wait_ge(weights_loaded, 16 * N_WEIGHTS)
            turned = 0

            def turned_in(rows, cols):
                nonlocal turned
                turned += 1
                dve.wait_ge(w_turned, turned)
                return psum[0:cols, (turned - 1) % 8, 0:rows]

            for t in range(3 * KC):
                for k in range(KC):
                    nc.vector.tensor_scalar(wqkvT[:, k, t * P:(t + 1) * P], turned_in(P, P), gamma_col[:, k:k + 1],
                                            None, ALU.mult).then_inc(w_kept, 1)
            for dst in (woutT, whT):
                for t in range(KC):
                    for k in range(KC):
                        nc.vector.tensor_copy(dst[:, k, t * P:(t + 1) * P], turned_in(P, P)).then_inc(w_kept, 1)
            for t in range(2):
                for k in range(KC):
                    src = turned_in(C8, P)
                    for part in range(KS // HD):
                        last = nc.vector.tensor_copy(wfgT[:, k, t, part * HD:(part + 1) * HD], src)
                    last.then_inc(w_kept, 1)
            nc.vector.tensor_copy(w0T, turned_in(D0, 2)).then_inc(w_kept, 1)
            nc.vector.tensor_copy(w1T, turned_in(D0, D0)).then_inc(w_kept, 1)
            nc.vector.tensor_copy(w2T, turned_in(G * HG, D0)).then_inc(w_kept, 1)
            def do(kind, arg, b, g, first, last, tail=False):
                if kind == "centre":
                    need(dve, "mean_mm", b, 1)
                    for k in range(KC):
                        nc.vector.tensor_tensor(xn[:, k, :], xn[:, k, :], pair(6),
                                                ALU.subtract).then_inc(SEMS["centered"], 1)
                elif kind == "norm":
                    if arg == 0:
                        need(dve, "rstd_ready", b, 2)
                        need(dve, "centered", b, KC)
                    nc.vector.tensor_tensor(xn[:, arg, :], xn[:, arg, :], rstd, ALU.mult).then_inc(SEMS["normed"], 1)
                elif kind == "low_q":
                    need(dve, "hi_ready", b, split(1, 0))
                    nc.vector.scalar_tensor_tensor(st[:, 1, ::-1], pair(6), SCALE, st[:, 0, ::-1].bitcast(F32),
                                                   ALU.mult, ALU.subtract).then_inc(SEMS["lo_ready"], 1)
                elif kind == "low_k":
                    need(dve, "hi_ready", b, split(1, 1))
                    nc.vector.tensor_tensor(st[:, 1, :], pair(6), st[:, 0, :].bitcast(F32),
                                            ALU.subtract).then_inc(SEMS["lo_ready"], 1)
                elif kind == "low_q0":
                    need(dve, "hi_ready", b, split(0, 0, arg))
                    nc.vector.scalar_tensor_tensor(back(st[:, 1, :], arg * HALF, HALF, N), psum[:, 5, :], SCALE,
                                                   back(st[:, 0, :], arg * HALF, HALF, N).bitcast(F32),
                                                   ALU.mult, ALU.subtract).then_inc(SEMS["lo_ready"], 1)
                elif kind == "low_k0":
                    cols = slice(arg * HALF, (arg + 1) * HALF)
                    need(dve, "hi_ready", b, split(0, 1, arg))
                    nc.vector.tensor_tensor(st[:, 1, cols], psum[:, 5 - arg, :], st[:, 0, cols].bitcast(F32),
                                            ALU.subtract).then_inc(SEMS["lo_ready"], 1)
                elif kind == "add_x":
                    c, half = divmod(arg, NHALF)
                    cols = slice(half * HALF, (half + 1) * HALF)
                    if arg == 0:
                        need(dve, "res_loaded", b, 16)
                    need(dve, "proj_mm", b, arg + 1)
                    nc.vector.tensor_tensor(x1[:, c, cols], x1[:, c, cols], psum[:, 4 + arg % 2, :],
                                            ALU.add).then_inc(SEMS["x1_ready"], 1)
                elif kind in ("low_f", "low_g"):
                    t = ("low_f", "low_g").index(kind)
                    rows = slice((2 - t) * HD, (3 - t) * HD)
                    cols = slice(arg * HALF, (arg + 1) * HALF) if t else slice(0, N)
                    src = psum[rows, 5, :] if t else pair(4)[rows]
                    need(dve, "fg_hi", b, t + arg + 1)
                    nc.vector.scalar_tensor_tensor(fg_stack[rows, t, cols], src, bfg[rows, t:t + 1],
                                                   fg_stack[rows, t, cols].bitcast(F32), ALU.add,
                                                   ALU.subtract).then_inc(SEMS["fg_lo"], 1)
                elif kind == "shift":
                    u = g * NHALF + arg
                    cols = slice(arg * HM, (arg + 1) * HM)
                    need(dve, "a_max", b, g * A_TILES + (arg + 1) * HM)
                    need(dve, "ln_ready", b, 2 * u + 2)
                    need(dve, "shift_mm", b, u - 1)
                    nc.vector.tensor_tensor(invsum[:, cols], rowsum[:, cols], invsum[:, cols],
                                            ALU.mult).then_inc(SEMS["scaled"], 1)
                    need(dve, "scaled", b, u + 1)
                    nc.vector.scalar_tensor_tensor(lnsum[:, cols], invsum[:, cols], -1.0, lnsum[:, cols],
                                                   ALU.add, ALU.add).then_inc(SEMS["shifted"], 1)
                    need(dve, "shifted", b, 2 * u + 1)
                    nc.vector.tensor_tensor(shift[:, cols], nmax[:, cols], lnsum[:, cols],
                                            ALU.subtract).then_inc(SEMS["shifted"], 1)
                    need(dve, "shifted", b, 2 * u + 2)
                    nc.vector.tensor_copy(shift_hi[:, cols], shift[:, cols]).then_inc(SEMS["split_hi"], 1)
                    need(dve, "split_hi", b, u + 1)
                    nc.vector.tensor_copy(shift_parts[:, arg, 0], shift_hi[:, cols].bitcast(F32))
                    nc.vector.tensor_tensor(shift_parts[:, arg, 1], shift[:, cols], shift_hi[:, cols].bitcast(F32),
                                            ALU.subtract).then_inc(SEMS["parts_ready"], 1)
                elif kind == "keep_h":
                    if arg == 0:
                        need(dve, "pv_mm", b + 1, 0 if tail else TG)
                    need(dve, "h_mm", b, arg + 1)
                    nc.vector.tensor_tensor(hT[:, arg, :], psum[:, 6 + arg % 2, 0:C], bh_all[:],
                                            ALU.add).then_inc(SEMS["h_ready"], 1)
                elif kind == "max1":
                    bank = 2 * (arg % 2) if tail else bank_of(g, first, ("s1", arg))
                    if arg == 0:
                        need(dve, "pv_mm", b + 1, 0 if tail else TG)
                    elif arg == 2 and not tail and not last:
                        need(dve, "normed", b + 2, KC)
                    elif arg >= 3:
                        need(dve, "sa_mm", b, arg - 2)
                    need(dve, "s1_mm", b, arg + 1)
                    nc.vector.tensor_scalar(attn1[arg % 3], pair(bank), -1.0, BIG, ALU.mult, ALU.min,
                                            accum_out=nmax1[:, arg:arg + 1]).then_inc(SEMS["nmax1_ready"], 1)
                elif kind == "invert":
                    need(dve, "e1_ready", b, arg + 1)
                    nc.vector.reciprocal(rl1[:, arg:arg + 1], l1[:, arg:arg + 1]).then_inc(SEMS["rl1_ready"], 1)
                elif kind == "add_y":
                    if arg == 0:
                        need(dve, "sa_mm", b, NT)
                    c, half = divmod(arg, NHALF)
                    c = KC - 1 - c
                    cols = slice(half * HALF, (half + 1) * HALF)
                    nc.vector.scalar_tensor_tensor(x1[:, c, cols], psum[:, 4 + 2 * c + half, :],
                                                   gamma1_col[:, 0:1], x1[:, c, cols], ALU.mult,
                                                   ALU.add).then_inc(SEMS["y_ready"], 1)

            for step in range(MSTEPS + 2):
                m = step
                if m < MSTEPS:
                    dve.wait_ge(hidden1_sum, m + 1)
                    if m >= 2:
                        dve.wait_ge(hidden2_mm, m - 1)
                    nc.vector.scalar_tensor_tensor(hidden1[:, m % 2], sum1[:, m % 2], LEAK, sum1[:, m % 2],
                                                   ALU.mult, ALU.max).then_inc(hidden1_ready, 1)
                m = step - 1
                if 0 <= m < MSTEPS:
                    dve.wait_ge(hidden2_sum, m + 1)
                    if m >= 2:
                        dve.wait_ge(table_mm, m - 1)
                    nc.vector.scalar_tensor_tensor(hidden2[:, m % 2], sum2[:, m % 2], LEAK, sum2[:, m % 2],
                                                   ALU.mult, ALU.max).then_inc(hidden2_ready, 1)
                m = step - 2
                if m >= 0:
                    dve.wait_ge(table_mm, m + 1)
                    nc.vector.tensor_scalar(table_sb[:, m * MC:(m + 1) * MC], psum[0:G * HG, 4 + m % 2, 0:MC],
                                            b2_col, None, ALU.add).then_inc(table_ready, 1)
                for at, kind, arg in ((2, "centre", 0), (6, "norm", 0), (6, "norm", 1)):
                    if step == at:
                        do(kind, arg, 0, 1, True, False)
            for kind, arg in (("low_k0", 0), ("low_k0", 1), ("low_q0", 0), ("low_q0", 1)):
                do(kind, arg, 0, 1, True, False)

            def element(b, first, last):
                for g in range(G):
                    for m in range(A_TILES):
                        r, h, t = row_tile(m)
                        a0 = (H - ROWS - ROWS * t) * W
                        free = (("sum_ready", b, g * A_TILES + m - BIASED + 1) if m >= BIASED else
                                ("probs_ready", b, (g - 1) * SN + last_in_slot(m)))
                        need_beside(dve, (lines_loaded[g * HG + h], 16 * ROWS), ("a_mm", b, g * A_TILES + m + 1), free)
                        nc.vector.tensor_tensor_reduce(biased[:, m % BIASED, :], pair(bank_of(g, first, ("rows", m))),
                                                       bias_lines[:, g * HG + h, a0:a0 + N], -1.0, BIG, ALU.add,
                                                       ALU.min, nmax[:, m:m + 1]).then_inc(SEMS["a_max"], 1)
                        for kind, arg, e in side_work(g, "rows", m, b, first, last):
                            do(kind, arg, e, g, first, last)
                    for n in range(SN):
                        half, t, j = column_tile(n)
                        a0 = (half * (H // NHALF) - ROWS * t + H - ROWS) * W
                        need(dve, "s_mm", b, g * SN + n + 1)
                        if n >= BIASED:
                            need(dve, "probs_ready", b, g * SN + n - BIASED + 1)
                        else:
                            need(dve, "sum_ready", b, g * A_TILES + last_in_slot(n))
                        bank = bank_of(g, first, ("columns", n))
                        nc.vector.tensor_tensor(biased[:, n % BIASED, :].rearrange("p (i n) -> p i n", i=2),
                                                psum[:, bank:bank + 2, :],
                                                bias_lines[:, g * HG + 2 * j:g * HG + 2 * j + 2, a0:a0 + HALF],
                                                ALU.add).then_inc(SEMS["bias_added"], 1)
                        for kind, arg, e in side_work(g, "columns", n, b, first, last):
                            do(kind, arg, e, g, first, last)

            batches(dve, element)
            for kind, arg, b in alone(LAYER_1):
                do(kind, arg, b, 1, False, False, tail=True)


N_WEIGHTS = 16 + 6


def back(ap, start, count, total):
    first = total - 1 - start
    stop = first - count
    return ap[:, first:(stop if stop >= 0 else None):-1]


def tiles_to_turn(square, narrow, small):
    for raw in square:
        for t in range(raw.shape[1]):
            for k in range(raw.shape[2] // P):
                yield raw[:, t, k * P:(k + 1) * P]
    for raw in narrow:
        for k in range(raw.shape[1] // P):
            yield raw[:, k * P:(k + 1) * P]
    yield from small


_INS = ["x", "L0_conv_gamma", "L0_conv_w_qkv", "L0_conv_w_out", "L0_conv_cpb_w0", "L0_conv_cpb_b0",
        "L0_conv_cpb_w1", "L0_conv_cpb_b1", "L0_conv_cpb_w2", "L0_conv_cpb_b2", "L1_conv_Wf", "L1_conv_bf",
        "L1_conv_Wg", "L1_conv_bg", "L1_conv_Wh", "L1_conv_bh", "L1_conv_gamma"]
_OUTS = [((8, 256, 32, 32), "float32")]


def shape_constants(side):
    d = np.arange(1 - side, side, dtype=np.float32)
    line = (np.sign(d) * np.log(np.abs(d) + np.float32(1.0))).astype(np.float32)
    dy, dx = np.meshgrid(line, line, indexing="ij")
    return [np.stack([dy.ravel(), dx.ravel()]), np.eye(P, dtype=np.float32)]


def kernel(**inputs):
    import concourse.bacc as bacc
    from concourse.bass_utils import run_bass_kernel_spmd

    nc = bacc.Bacc("TRN2", target_bir_lowering=False, num_devices=1)
    arrays, args = {}, []
    named = [(n, np.ascontiguousarray(inputs[n])) for n in _INS]
    named += list(zip(("rel_log", "identity"), shape_constants(inputs["x"].shape[2])))
    for name, a in named:
        arrays[f"in_{name}_dram"] = a
        args.append(nc.dram_tensor(f"in_{name}_dram", a.shape, mybir.dt.from_np(a.dtype), kind="ExternalInput").ap())
    for i, (shape, dtype) in enumerate(_OUTS):
        args.append(nc.dram_tensor(f"out_{i}_dram", shape, mybir.dt.from_np(np.dtype(dtype)),
                                   kind="ExternalOutput").ap())
    two_layer_attention(nc, *args)
    r = run_bass_kernel_spmd(nc, [arrays], core_ids=[0])
    return r.results[0]["out_0_dram"]
```
